# Optimizing a Trainium2 kernel written in Bass

```python
import numpy as np
import jax
import jax.numpy as jnp

def _softmax(x, axis=-1):
    return jax.nn.softmax(x, axis=axis)

def _gelu(x):
    return jax.nn.gelu(x, approximate=True)

def _silu(x):
    return jax.nn.silu(x)

def _sigmoid(x):
    return jax.nn.sigmoid(x)

def _layernorm(x, axis=-1, eps=1e-05):
    m = jnp.mean(x, axis=axis, keepdims=True)
    v = jnp.var(x, axis=axis, keepdims=True)
    return (x - m) / jnp.sqrt(v + eps)

def _scatter_add(tgt, idx, src, axis=0):
    return tgt.at[idx].add(src)

def _segment_sum(src, seg, n):
    return jax.ops.segment_sum(src, seg, n)
kernel_name = 'mk_xattn_seq_d1_seqx_r8_4beb77'

def setup_inputs(seed: int=0):
    np.random.seed(seed)
    _w = jnp.asarray

    def _rec_inputs():
        import jax
        import jax.numpy as jnp
        _rk = jax.random.key(seed)
        x = -0.0002928 + 1 * jax.random.normal(jax.random.fold_in(_rk, 1), (16, 64, 128), jnp.float32)
        _lenS = 64 - jax.random.randint(jax.random.fold_in(_rk, 7), (16,), 0, max(1, 64 // 4) + 1, jnp.int32)
        _lenS2 = 64 - jax.random.randint(jax.random.fold_in(_rk, 8), (16,), 0, max(1, 64 // 4) + 1, jnp.int32)
        _ctx_1024P = jax.random.normal(jax.random.fold_in(_rk, 11), (16, 16, 128), jnp.float32)
        _ctx_1024c = jax.random.dirichlet(jax.random.fold_in(_rk, 511), 0.3 * jnp.ones((16,), jnp.float32), (16, 64))
        _ctx_1024t = jnp.einsum('bsk,bkd->bsd', _ctx_1024c, _ctx_1024P)
        _ctx_1024t = _ctx_1024t * jax.lax.rsqrt(jnp.mean(jnp.square(_ctx_1024t)) + 1e-12) * 0.953939
        ctx_1024 = -1.39393e-06 + 0.999914 * (_ctx_1024t + 0.3 * jax.random.normal(jax.random.fold_in(_rk, 611), (16, 64, 128), jnp.float32))
        return (x, ctx_1024)
    x, ctx_1024 = _rec_inputs()

    def _L0_xattn_setup():
        import jax, jax.numpy as jnp
        import numpy as np
        B, S, SE, D, H, FF, E, K = (2, 256, 256, 128, 16, 512, 8, 2)
        HD = D // H

        def _layernorm(x, g, b):
            m = x.mean(-1, keepdims=True)
            v = ((x - m) ** 2).mean(-1, keepdims=True)
            return (x - m) / jnp.sqrt(v + 1e-05) * g + b

        def _attn(q_in, k_in, v_in, wq, bq, wk, bk, wv, bv, wo, bo, causal):
            Bq, Sq, Dm = q_in.shape
            Sk = k_in.shape[1]
            Q = (q_in @ wq + bq).reshape(Bq, Sq, H, HD)
            Kp = (k_in @ wk + bk).reshape(Bq, Sk, H, HD)
            V = (v_in @ wv + bv).reshape(Bq, Sk, H, HD)
            scores = jnp.einsum('bqhd,bkhd->bhqk', Q, Kp) / jnp.sqrt(jnp.float32(HD))
            if causal:
                mask = jnp.tril(jnp.ones((Sq, Sk), bool))
                scores = jnp.where(mask, scores, -jnp.inf)
            a = jax.nn.softmax(scores, axis=-1)
            o = jnp.einsum('bhqk,bkhd->bqhd', a, V).reshape(Bq, Sq, Dm)
            return o @ wo + bo

        def _moe(x, rw, rb, w1, b1, w2, b2):
            T = x.shape[0] * x.shape[1]
            xf = x.reshape(T, D)
            router_weights = jax.nn.softmax(xf @ rw + rb, axis=-1)
            topw, topi = jax.lax.top_k(router_weights, K)
            topw = jax.nn.softmax(topw, axis=-1)
            combine = jnp.zeros((T, E), xf.dtype).at[jnp.arange(T)[:, None], topi].add(topw)
            h = jax.nn.gelu(jnp.einsum('td,edf->etf', xf, w1) + b1[:, None, :], approximate=False)
            eo = jnp.einsum('etf,efd->etd', h, w2) + b2[:, None, :]
            out = jnp.einsum('etd,te->td', eo, combine)
            return out.reshape(x.shape)
        key = jax.random.key(seed)
        ks = jax.random.split(key, 32)
        w = lambda k, shape: jax.random.normal(k, shape, jnp.float32) * 0.02
        inp = {'x': jax.random.normal(ks[0], (B, S, D), jnp.float32), 'encoder_output': jax.random.normal(ks[1], (B, SE, D), jnp.float32), 'sa_wq': w(ks[2], (D, D)), 'sa_bq': jnp.zeros((D,), jnp.float32), 'sa_wk': w(ks[3], (D, D)), 'sa_bk': jnp.zeros((D,), jnp.float32), 'sa_wv': w(ks[4], (D, D)), 'sa_bv': jnp.zeros((D,), jnp.float32), 'sa_wo': w(ks[5], (D, D)), 'sa_bo': jnp.zeros((D,), jnp.float32), 'ca_wq': w(ks[6], (D, D)), 'ca_bq': jnp.zeros((D,), jnp.float32), 'ca_wk': w(ks[7], (D, D)), 'ca_bk': jnp.zeros((D,), jnp.float32), 'ca_wv': w(ks[8], (D, D)), 'ca_bv': jnp.zeros((D,), jnp.float32), 'ca_wo': w(ks[9], (D, D)), 'ca_bo': jnp.zeros((D,), jnp.float32), 'ln1_g': jnp.ones((D,), jnp.float32), 'ln1_b': jnp.zeros((D,), jnp.float32), 'ln2_g': jnp.ones((D,), jnp.float32), 'ln2_b': jnp.zeros((D,), jnp.float32), 'ln3_g': jnp.ones((D,), jnp.float32), 'ln3_b': jnp.zeros((D,), jnp.float32), 'router_w': w(ks[10], (D, E)), 'router_b': jnp.zeros((E,), jnp.float32), 'e_w1': w(ks[11], (E, D, FF)), 'e_b1': jnp.zeros((E, FF), jnp.float32), 'e_w2': w(ks[12], (E, FF, D)), 'e_b2': jnp.zeros((E, D), jnp.float32)}
        return inp
    _L0_xattn_all = _L0_xattn_setup()
    _L0_xattn_in = {k: v for k, v in _L0_xattn_all.items() if k in ('sa_wq', 'sa_bq', 'sa_wk', 'sa_bk', 'sa_wv', 'sa_bv', 'sa_wo', 'sa_bo', 'ca_wq', 'ca_bq', 'ca_wk', 'ca_bk', 'ca_wv', 'ca_bv', 'ca_wo', 'ca_bo', 'ln1_g', 'ln1_b', 'ln2_g', 'ln2_b', 'ln3_g', 'ln3_b', 'router_w', 'router_b', 'e_w1', 'e_b1', 'e_w2', 'e_b2')}
    del _L0_xattn_all
    return {'x': x, 'ctx_1024': ctx_1024, 'L0_xattn_sa_wq': _L0_xattn_in['sa_wq'], 'L0_xattn_sa_bq': _L0_xattn_in['sa_bq'], 'L0_xattn_sa_wk': _L0_xattn_in['sa_wk'], 'L0_xattn_sa_bk': _L0_xattn_in['sa_bk'], 'L0_xattn_sa_wv': _L0_xattn_in['sa_wv'], 'L0_xattn_sa_bv': _L0_xattn_in['sa_bv'], 'L0_xattn_sa_wo': _L0_xattn_in['sa_wo'], 'L0_xattn_sa_bo': _L0_xattn_in['sa_bo'], 'L0_xattn_ca_wq': _L0_xattn_in['ca_wq'], 'L0_xattn_ca_bq': _L0_xattn_in['ca_bq'], 'L0_xattn_ca_wk': _L0_xattn_in['ca_wk'], 'L0_xattn_ca_bk': _L0_xattn_in['ca_bk'], 'L0_xattn_ca_wv': _L0_xattn_in['ca_wv'], 'L0_xattn_ca_bv': _L0_xattn_in['ca_bv'], 'L0_xattn_ca_wo': _L0_xattn_in['ca_wo'], 'L0_xattn_ca_bo': _L0_xattn_in['ca_bo'], 'L0_xattn_ln1_g': _L0_xattn_in['ln1_g'], 'L0_xattn_ln1_b': _L0_xattn_in['ln1_b'], 'L0_xattn_ln2_g': _L0_xattn_in['ln2_g'], 'L0_xattn_ln2_b': _L0_xattn_in['ln2_b'], 'L0_xattn_ln3_g': _L0_xattn_in['ln3_g'], 'L0_xattn_ln3_b': _L0_xattn_in['ln3_b'], 'L0_xattn_router_w': _L0_xattn_in['router_w'], 'L0_xattn_router_b': _L0_xattn_in['router_b'], 'L0_xattn_e_w1': _L0_xattn_in['e_w1'], 'L0_xattn_e_b1': _L0_xattn_in['e_b1'], 'L0_xattn_e_w2': _L0_xattn_in['e_w2'], 'L0_xattn_e_b2': _L0_xattn_in['e_b2']}

def reference(x, ctx_1024, L0_xattn_sa_wq, L0_xattn_sa_bq, L0_xattn_sa_wk, L0_xattn_sa_bk, L0_xattn_sa_wv, L0_xattn_sa_bv, L0_xattn_sa_wo, L0_xattn_sa_bo, L0_xattn_ca_wq, L0_xattn_ca_bq, L0_xattn_ca_wk, L0_xattn_ca_bk, L0_xattn_ca_wv, L0_xattn_ca_bv, L0_xattn_ca_wo, L0_xattn_ca_bo, L0_xattn_ln1_g, L0_xattn_ln1_b, L0_xattn_ln2_g, L0_xattn_ln2_b, L0_xattn_ln3_g, L0_xattn_ln3_b, L0_xattn_router_w, L0_xattn_router_b, L0_xattn_e_w1, L0_xattn_e_b1, L0_xattn_e_w2, L0_xattn_e_b2):
    import jax
    import jax.numpy as jnp

    def _L0_xattn_ref(x, encoder_output, sa_wq, sa_bq, sa_wk, sa_bk, sa_wv, sa_bv, sa_wo, sa_bo, ca_wq, ca_bq, ca_wk, ca_bk, ca_wv, ca_bv, ca_wo, ca_bo, ln1_g, ln1_b, ln2_g, ln2_b, ln3_g, ln3_b, router_w, router_b, e_w1, e_b1, e_w2, e_b2):
        import jax, jax.numpy as jnp
        import numpy as np
        B, S, SE, D, H, FF, E, K = (2, 256, 256, 128, 16, 512, 8, 2)
        HD = D // H

        def _layernorm(x, g, b):
            m = x.mean(-1, keepdims=True)
            v = ((x - m) ** 2).mean(-1, keepdims=True)
            return (x - m) / jnp.sqrt(v + 1e-05) * g + b

        def _attn(q_in, k_in, v_in, wq, bq, wk, bk, wv, bv, wo, bo, causal):
            Bq, Sq, Dm = q_in.shape
            Sk = k_in.shape[1]
            Q = (q_in @ wq + bq).reshape(Bq, Sq, H, HD)
            Kp = (k_in @ wk + bk).reshape(Bq, Sk, H, HD)
            V = (v_in @ wv + bv).reshape(Bq, Sk, H, HD)
            scores = jnp.einsum('bqhd,bkhd->bhqk', Q, Kp) / jnp.sqrt(jnp.float32(HD))
            if causal:
                mask = jnp.tril(jnp.ones((Sq, Sk), bool))
                scores = jnp.where(mask, scores, -jnp.inf)
            a = jax.nn.softmax(scores, axis=-1)
            o = jnp.einsum('bhqk,bkhd->bqhd', a, V).reshape(Bq, Sq, Dm)
            return o @ wo + bo

        def _moe(x, rw, rb, w1, b1, w2, b2):
            T = x.shape[0] * x.shape[1]
            xf = x.reshape(T, D)
            router_weights = jax.nn.softmax(xf @ rw + rb, axis=-1)
            topw, topi = jax.lax.top_k(router_weights, K)
            topw = jax.nn.softmax(topw, axis=-1)
            combine = jnp.zeros((T, E), xf.dtype).at[jnp.arange(T)[:, None], topi].add(topw)
            h = jax.nn.gelu(jnp.einsum('td,edf->etf', xf, w1) + b1[:, None, :], approximate=False)
            eo = jnp.einsum('etf,efd->etd', h, w2) + b2[:, None, :]
            out = jnp.einsum('etd,te->td', eo, combine)
            return out.reshape(x.shape)
        x = _layernorm(x + _attn(x, x, x, sa_wq, sa_bq, sa_wk, sa_bk, sa_wv, sa_bv, sa_wo, sa_bo, True), ln1_g, ln1_b)
        x = _layernorm(x + _attn(x, encoder_output, encoder_output, ca_wq, ca_bq, ca_wk, ca_bk, ca_wv, ca_bv, ca_wo, ca_bo, False), ln2_g, ln2_b)
        x = _layernorm(x + _moe(x, router_w, router_b, e_w1, e_b1, e_w2, e_b2), ln3_g, ln3_b)
        return x
    x = _L0_xattn_ref(x, ctx_1024, L0_xattn_sa_wq, L0_xattn_sa_bq, L0_xattn_sa_wk, L0_xattn_sa_bk, L0_xattn_sa_wv, L0_xattn_sa_bv, L0_xattn_sa_wo, L0_xattn_sa_bo, L0_xattn_ca_wq, L0_xattn_ca_bq, L0_xattn_ca_wk, L0_xattn_ca_bk, L0_xattn_ca_wv, L0_xattn_ca_bv, L0_xattn_ca_wo, L0_xattn_ca_bo, L0_xattn_ln1_g, L0_xattn_ln1_b, L0_xattn_ln2_g, L0_xattn_ln2_b, L0_xattn_ln3_g, L0_xattn_ln3_b, L0_xattn_router_w, L0_xattn_router_b, L0_xattn_e_w1, L0_xattn_e_b1, L0_xattn_e_w2, L0_xattn_e_b2)
    return x

_drawn_inputs = setup_inputs


def setup_inputs(seed=0):
    import zlib

    import numpy as np

    out = dict(_drawn_inputs(seed))
    spreads = {'L0_xattn_sa_bq': (0.0, 0.8),
     'L0_xattn_sa_bk': (0.0, 2.0),
     'L0_xattn_sa_bv': (0.0, 0.1),
     'L0_xattn_sa_bo': (0.0, 0.1),
     'L0_xattn_ca_bq': (0.0, 2.0),
     'L0_xattn_ca_bk': (0.0, 2.0),
     'L0_xattn_ca_bv': (0.0, 0.311),
     'L0_xattn_ca_bo': (0.0, 0.1),
     'L0_xattn_ln1_g': (1.0, 0.2),
     'L0_xattn_ln1_b': (0.0, 0.1),
     'L0_xattn_ln2_g': (1.0, 0.2),
     'L0_xattn_ln2_b': (0.0, 0.1),
     'L0_xattn_ln3_g': (1.0, 0.2),
     'L0_xattn_ln3_b': (0.0, 0.1),
     'L0_xattn_router_b': (0.0, 0.1),
     'L0_xattn_e_b1': (0.0, 0.517),
     'L0_xattn_e_b2': (0.0, 0.1)}
    factors = {'L0_xattn_sa_wq': 8.0,
     'L0_xattn_sa_wk': 8.0,
     'L0_xattn_sa_wv': 3.289,
     'L0_xattn_ca_wq': 8.0,
     'L0_xattn_ca_wk': 8.0}
    for name, (base, spread) in spreads.items():
        noise = np.random.default_rng([zlib.crc32(name.encode()), seed]).standard_normal(out[name].shape)
        drawn = base * np.exp(spread * noise) if base else spread * noise
        out[name] = jnp.asarray(drawn.astype(out[name].dtype))
    for name, factor in factors.items():
        out[name] = (out[name] * factor).astype(out[name].dtype)
    return out
```

```python
from contextlib import ExitStack

import concourse.bass as bass
from concourse import mybir

F32 = mybir.dt.float32
BF16 = mybir.dt.bfloat16
ALU = mybir.AluOpType
ACT = mybir.ActivationFunctionType
AX = mybir.AxisListType

P = 128
D = 128
SEQ = 64
HEADS = 16
HD = D // HEADS
EPS = 1e-5
MASKED = -1e30
VW = HD + 1


def build_decoder_layer(nc, x, ctx, sa, ca, ln, router_w, router_b, w1, b1, w2, b2, out):
    NSEQ = x.shape[0]
    TILES = NSEQ * SEQ // P
    UNITS = 2 * TILES
    E, _, FF = w1.shape
    FC = FF // P
    CH = 512
    CHUNKS = TILES * P // CH
    TPC = CH // P
    STEPS = CHUNKS * E
    SCALE = float(HD) ** -0.5
    SLOTS = 4
    HP = HEADS // 2
    SW = HEADS * SEQ

    x_tok = x.rearrange("(t b) s d -> (b s) t d", b=2)
    ctx_tok = ctx.rearrange("(t b) s d -> (b s) t d", b=2)
    out_tok = out.rearrange("(t b) s d -> (b s) t d", b=2)
    w1_v = w1.rearrange("e d f -> d e f")
    w2_v = w2.rearrange("e (k p) d -> p e k d", p=P)
    att = [sa, ca]

    with ExitStack() as stack:
        def sb(name, shape, dt=F32):
            return stack.enter_context(nc.sbuf_tensor(name, shape, dt))

        def ps(name, shape):
            return stack.enter_context(nc.psum_tensor(name, shape, F32))

        def sem(name):
            return stack.enter_context(nc.semaphore(name))

        scores_ps = ps("scores_ps", [P, 2, SW])
        probsT_ps = ps("probsT_ps", [P, 2, 512])
        act_ps = ps("act_ps", [P, 512])
        dve_ps = ps("dve_ps", [P, 512])

        x_sb = sb("x_sb", [P, TILES, D])
        ctx_sb = sb("ctx_sb", [P, TILES, D])
        srcT = sb("srcT", [P, 2, TILES * P])
        keysT = sb("keysT", [P, 2, NSEQ, SEQ])
        keys_bd = sb("keys_bd", [P, SLOTS, 2, SW])
        vals = sb("vals", [P, 2, NSEQ, HP, 2, VW])
        wqkvo = {(a, n): sb(f"w{n}{a}", [D, D]) for a in range(2) for n in "qkvo"}
        NROWS = 8 + E * FC
        rows = sb("rows", [NROWS, D])
        cols = sb("cols", [P, NROWS])
        COL = {n: i for i, n in enumerate(["bq0", "bk0", "bq1", "bk1", "g0", "b0", "g1", "b1"])}
        B1COL = 8
        bc = {n: sb(f"bc_{n}", [P, D]) for n in ["bv0", "bv1", "bo0", "bo1", "g0", "b0", "g1", "b1", "g2", "b2"]}
        b0bo1 = sb("b0bo1", [P, D])
        rb_bc = sb("rb_bc", [P, E])
        rw_sb = sb("rw_sb", [D, E])
        b2_bd = sb("b2_bd", [TILES * E, TILES * D])
        ident = sb("ident", [P, P])
        ident_bf = sb("ident_bf", [P, P], BF16)
        mask_bf = sb("mask_bf", [P, 512], BF16)
        neg_half = sb("neg_half", [P, TILES])
        rank = sb("rank", [P, E])
        w1_sb = sb("w1_sb", [D, E, FF])
        w2_sb = sb("w2_sb", [P, E, FC, D])

        qT = sb("qT", [P, 2, P])
        top = sb("top", [P, 2, HEADS])
        probs = sb("probs", [P, 2, SW])
        probsT = sb("probsT", [P, 2, SW])
        rsum = sb("rsum", [P, 2, HEADS])
        mixed = sb("mixed", [P, 2, D])
        mixedT = sb("mixedT", [P, 2, P])
        summed = sb("summed", [P, 2, D])
        stats = sb("stats", [P, 2, 6])
        mv = sb("mv", [P, 2, 2])
        veps = sb("veps", [P, 2])
        rstd = sb("rstd", [P, 2])
        xn = sb("xn", [P, 2, D])
        gx = sb("gx", [P, D])
        res = sb("res", [P, 3, TILES, D])
        yT = sb("yT", [P, 2, TILES * P])
        h_sb = sb("h_sb", [P, 2 * FC, CH])
        r_buf = sb("r_buf", [P, 12, TILES, E])
        r_one = sb("r_one", [P, 8, TILES])
        gate = sb("gate", [P, TILES, E])
        gateT = sb("gateT", [TILES * E, P])
        acc = sb("acc", [P, TILES, D])
        st3 = sb("st3", [P, TILES, 6])
        mv3 = sb("mv3", [P, TILES, 2])
        ve3 = sb("ve3", [P, TILES])
        rstd3 = sb("rstd3", [P, TILES])
        y3 = sb("y3", [P, TILES, D])

        x_in, ctx_in, rows_in, small_in = sem("x_in"), sem("ctx_in"), sem("rows_in"), sem("small_in")
        wk_in, wv_in, wq_in = [[sem(f"{n}_in{a}") for a in range(2)] for n in ("wk", "wv", "wq")]
        bv_in = sem("bv_in")
        keys_in = [sem(f"keys_in{s}") for s in range(SLOTS)]
        w1_in = [sem(f"w1_in{e}") for e in range(E)]
        w2_in = [sem(f"w2_in{e}") for e in range(E)]
        zeroed_g, zeroed_v = sem("zeroed_g"), sem("zeroed_v")
        consts = sem("consts")
        pro_ready, pro_act, pro_dve = sem("pro_ready"), sem("pro_act"), sem("pro_dve")
        q_ready, q_used = sem("q_ready"), sem("q_used")
        scores_ready, max_ready, shifted = sem("scores_ready"), sem("max_ready"), sem("shifted")
        probs_ready, probsT_ready = sem("probs_ready"), sem("probsT_ready")
        probsT_act, probsT_dve = sem("probsT_act"), sem("probsT_dve")
        pv_ready, rsum_ready, mixed_ready = sem("pv_ready"), sem("rsum_ready"), sem("mixed_ready")
        mixedT_ready, mixedT_used = sem("mixedT_ready"), sem("mixedT_used")
        proj_ready, summed_ready, stats_ready = sem("proj_ready"), sem("summed_ready"), sem("stats_ready")
        mv_ready, veps_ready, rstd_ready = sem("mv_ready"), sem("veps_ready"), sem("rstd_ready")
        xn_ready, xnT_ready, yT_ready = sem("xn_ready"), sem("xnT_ready"), sem("yT_ready")
        res0_ready, gx_ready, res_ready = sem("res0_ready"), sem("gx_ready"), sem("res_ready")
        logits_ready, rchain, r_exp_in, r_exp = sem("logits_ready"), sem("rchain"), sem("r_exp_in"), sem("r_exp")
        gate_ready, gateT_ready, gateT_used, b2_ready = sem("gate_ready"), sem("gateT_ready"), sem("gateT_used"), sem("b2_ready")
        up_ready, gelu_ready, down_ready, acc_ready = sem("up_ready"), sem("gelu_ready"), sem("down_ready"), sem("acc_ready")
        l3chain, ve3_ready, rstd3_ready, y3_ready, y3g_ready, y_ready, stored = (
            sem("l3chain"), sem("ve3_ready"), sem("rstd3_ready"), sem("y3_ready"), sem("y3g_ready"), sem("y_ready"), sem("stored"))
        chain_g, b2_in = sem("chain_g"), sem("b2_in")

        opening = []
        for a in range(2):
            opening += [("T", a, 0, "act"), ("T", a, 1, "dve"), ("K", a, 0, "act"), ("K", a, 1, "act")]
            opening += [("V", a, g, "dve") for g in range(4)]
        NB = 6

        def open_bank(n):
            b = n % NB
            return scores_ps[:, b // 2, (b % 2) * 512:(b % 2) * 512 + 512] if b < 4 else probsT_ps[:, b - 4, :]

        def read_count(n):
            who = opening[n][3]
            return (pro_act if who == "act" else pro_dve), sum(o[3] == who for o in opening[:n + 1])

        def product(what, a, part):
            return next(n for n, o in enumerate(opening) if o[:3] == (what, a, part))

        PRO_ACT = sum(o[3] == "act" for o in opening)
        PRO_DVE = len(opening) - PRO_ACT

        block = stack.enter_context(nc.Block())

        @block.sync
        def _(sp):
            half = TILES // 2
            sp.dma_start(x_sb[:, 0:half, :], x_tok[:, 0:half, :]).then_inc(x_in, 16)
            sp.dma_start(x_sb[:, half:, :], x_tok[:, half:, :]).then_inc(x_in, 16)
            sp.dma_start(wqkvo[0, "k"][:], sa["wk"]).then_inc(wk_in[0], 16)
            sp.dma_start(wqkvo[0, "v"][:], sa["wv"]).then_inc(wv_in[0], 16)
            sp.dma_start(wqkvo[0, "q"][:], sa["wq"]).then_inc(wq_in[0], 16)
            sp.dma_start(ctx_sb[:, 0:half, :], ctx_tok[:, 0:half, :]).then_inc(ctx_in, 16)
            sp.dma_start(ctx_sb[:, half:, :], ctx_tok[:, half:, :]).then_inc(ctx_in, 16)
            sp.dma_start(wqkvo[1, "k"][:], ca["wk"]).then_inc(wk_in[1], 16)
            sp.dma_start(wqkvo[1, "v"][:], ca["wv"]).then_inc(wv_in[1], 16)
            sp.dma_start(wqkvo[1, "q"][:], ca["wq"]).then_inc(wq_in[1], 16)
            sp.wait_ge(zeroed_g, 2)
            sp.wait_ge(zeroed_v, 2)
            for u in range(UNITS):
                a, t, slot = u // TILES, u % TILES, u % SLOTS
                s, v = read_count(product("K", a, t // (TILES // 2)))
                sp.wait_ge(s, v)
                if u >= SLOTS:
                    sp.wait_ge(scores_ready, u - SLOTS + 1)
                for h in range(HEADS):
                    sp.dma_start(keys_bd[h * HD:(h + 1) * HD, slot, :, h * SEQ:(h + 1) * SEQ],
                                 keysT[h * HD:(h + 1) * HD, a, 2 * t:2 * t + 2, :]).then_inc(keys_in[slot], 16)
                if u < E:
                    sp.dma_start(w1_sb[:, u, :], w1_v[:, u, :]).then_inc(w1_in[u], 16)
                elif u - E < E:
                    sp.dma_start(w2_sb[:, u - E, :, :], w2_v[:, u - E, :, :]).then_inc(w2_in[u - E], 16)
            for c in range(CHUNKS):
                sp.wait_ge(y_ready, c + 1)
                sp.dma_start(out_tok[:, c * TPC:(c + 1) * TPC, :], y3[:, c * TPC:(c + 1) * TPC, :]).then_inc(stored, 16)
            sp.wait_ge(stored, 16 * CHUNKS)

        @block.scalar
        def _(act):
            vecs = [sa["bq"], sa["bk"], ca["bq"], ca["bk"], ln[0][0], ln[0][1], ln[1][0], ln[1][1]]
            for i, v in enumerate(vecs):
                act.dma_start(rows[i:i + 1, :], v.rearrange("(a d) -> a d", a=1)).then_inc(rows_in, 16)
            act.dma_start(rows[8:8 + E * FC, :], b1.rearrange("e (k f) -> (e k) f", f=P)).then_inc(rows_in, 16)
            for a in range(2):
                act.dma_start(bc[f"bv{a}"][:], att[a]["bv"].partition_broadcast(P)).then_inc(bv_in, 16)
            for a in range(2):
                act.dma_start(bc[f"bo{a}"][:], att[a]["bo"].partition_broadcast(P)).then_inc(small_in, 16)
                act.dma_start(wqkvo[a, "o"][:], att[a]["wo"]).then_inc(small_in, 16)
            for i in range(3):
                act.dma_start(bc[f"g{i}"][:], ln[i][0].partition_broadcast(P)).then_inc(small_in, 16)
                act.dma_start(bc[f"b{i}"][:], ln[i][1].partition_broadcast(P)).then_inc(small_in, 16)
            act.dma_start(rb_bc[:], router_b.partition_broadcast(P)).then_inc(small_in, 16)
            act.dma_start(rw_sb[:], router_w).then_inc(small_in, 16)

            act.wait_ge(q_ready, 1)
            nc.scalar.copy(cols[:], act_ps[:, 0:NROWS]).then_inc(q_used, 1)
            act.wait_ge(q_used, 1)
            for n, (what, a, part, who) in enumerate(opening):
                if who != "act":
                    continue
                act.wait_ge(pro_ready, n + 1)
                if what == "T":
                    nc.scalar.copy(srcT[:, a, part * 512:part * 512 + 512], open_bank(n)).then_inc(pro_act, 1)
                else:
                    nc.scalar.activation(
                        keysT[:, a, part * 8:part * 8 + 8, :], open_bank(n).rearrange("p (b k) -> p b k", k=SEQ),
                        ACT.Identity, bias=cols[:, COL[f"bk{a}"]:COL[f"bk{a}"] + 1]).then_inc(pro_act, 1)

            def q_copy(u):
                c = COL[f"bq{u // TILES}"]
                act.wait_ge(q_ready, u + 2)
                if u >= 2:
                    act.wait_ge(scores_ready, u - 1)
                nc.scalar.activation(qT[:, u % 2, :], act_ps[:, 0:P], ACT.Identity,
                                     bias=cols[:, c:c + 1]).then_inc(q_used, 1)

            q_copy(0)
            for t in range(UNITS + 4):
                if t + 1 < UNITS:
                    q_copy(t + 1)
                u = t - 1
                if 0 <= u < UNITS:
                    act.wait_ge(probsT_ready, 2 * u + 1)
                    if u >= 2:
                        act.wait_ge(pv_ready, u - 1)
                    nc.scalar.copy(probsT[:, u % 2, 0:512], probsT_ps[:, 0, :]).then_inc(probsT_act, 1)
                if t < UNITS:
                    act.wait_ge(shifted, t + 1)
                    nc.scalar.activation(probs[:, t % 2, :], probs[:, t % 2, :], ACT.Exp,
                                         scale=SCALE).then_inc(probs_ready, 1)
                u = t - 3
                if 0 <= u < UNITS:
                    n, tile = u // TILES, u % TILES
                    act.wait_ge(xnT_ready, u + 1)
                    nc.scalar.activation(yT[:, n, tile * P:(tile + 1) * P], act_ps[:, 0:P], ACT.Identity,
                                         bias=cols[:, COL[f"b{n}"]:COL[f"b{n}"] + 1],
                                         scale=cols[:, COL[f"g{n}"]:COL[f"g{n}"] + 1]).then_inc(yT_ready, 1)
                u = t - 2
                if 0 <= u < UNITS:
                    act.wait_ge(mixedT_ready, u + 1)
                    if u >= 2:
                        act.wait_ge(proj_ready, u - 1)
                    nc.scalar.copy(mixedT[:, u % 2, :], dve_ps[:, 0:P]).then_inc(mixedT_used, 1)

            act.wait_ge(r_exp_in, 1)
            nc.scalar.activation(r_buf[:, 2], r_buf[:, 1], ACT.Exp).then_inc(r_exp, 1)
            act.wait_ge(r_exp_in, 2)
            nc.scalar.activation(r_one[:, 4], r_one[:, 3], ACT.Exp).then_inc(r_exp, 1)

            def gelus(g):
                e = g % E
                for k in range(FC):
                    n = g * FC + k
                    act.wait_ge(up_ready, n + 1)
                    if g >= 2:
                        act.wait_ge(down_ready, g - 1)
                    nc.scalar.activation(h_sb[:, n % (2 * FC), :], scores_ps[:, k // 2, (k % 2) * 512:(k % 2) * 512 + 512],
                                         ACT.Gelu, bias=cols[:, B1COL + e * FC + k:B1COL + e * FC + k + 1]).then_inc(gelu_ready, 1)

            for g in range(STEPS):
                gelus(g)
                if g == 1:
                    act.wait_ge(gateT_ready, 1)
                    nc.scalar.copy(gateT[:], act_ps[0:TILES * E, 128:256]).then_inc(gateT_used, 1)

        @block.tensor
        def _(pe):
            pe.wait_ge(consts, 3)
            pe.wait_ge(rows_in, 16 * 9)
            nc.tensor.transpose(act_ps[:, 0:NROWS], rows[:], ident[0:NROWS, 0:NROWS]).then_inc(q_ready, 1)
            src_sb = [x_sb, ctx_sb]
            src_in = [x_in, ctx_in]
            for n, (what, a, part, who) in enumerate(opening):
                if n >= NB:
                    s, v = read_count(n - NB)
                    pe.wait_ge(s, v)
                bank = open_bank(n)
                if what == "T":
                    pe.wait_ge(src_in[a], 32)
                    for j in range(4):
                        mm = nc.tensor.transpose(bank[:, j * P:(j + 1) * P], src_sb[a][:, part * 4 + j, :], ident[:])
                elif what == "K":
                    s, v = read_count(product("T", a, part))
                    pe.wait_ge(s, v)
                    pe.wait_ge(wk_in[a], 16)
                    mm = nc.tensor.matmul(bank, wqkvo[a, "k"][:], srcT[:, a, part * 512:part * 512 + 512],
                                          start=True, stop=True)
                else:
                    s, v = read_count(product("T", a, part // 2))
                    pe.wait_ge(s, v)
                    pe.wait_ge(wv_in[a], 16)
                    for j in range(4):
                        b = part * 4 + j
                        for r in range(2):
                            mm = nc.tensor.matmul(bank[r * SEQ:(r + 1) * SEQ, j * D:(j + 1) * D],
                                                  srcT[:, a, b * SEQ:(b + 1) * SEQ], wqkvo[a, "v"][:],
                                                  start=True, stop=True)
                mm.then_inc(pro_ready, 1)

            def q_product(u):
                a, tile = u // TILES, u % TILES
                if u == 0:
                    pe.wait_ge(q_used, 1)
                else:
                    pe.wait_ge(q_used, u + 1)
                if u - 5 >= 0:
                    pe.wait_ge(yT_ready, u - 4)
                pe.wait_ge(wq_in[a], 16)
                if a == 0:
                    rhs = srcT[:, 0, tile * P:(tile + 1) * P]
                else:
                    pe.wait_ge(yT_ready, tile + 1)
                    rhs = yT[:, 0, tile * P:(tile + 1) * P]
                nc.tensor.matmul(act_ps[:, 0:P], wqkvo[a, "q"][:], rhs, start=True, stop=True).then_inc(q_ready, 1)

            q_product(0)
            pe.wait_ge(pro_act, PRO_ACT)
            pe.wait_ge(pro_dve, PRO_DVE)
            pe.wait_ge(small_in, 16 * 12)
            for t in range(UNITS + 4):
                u = t - 3
                if 0 <= u < UNITS:
                    pe.wait_ge(mixedT_used, u + 1)
                    nc.tensor.matmul(dve_ps[:, 0:D], mixedT[:, u % 2, :], wqkvo[u // TILES, "o"][:],
                                     start=True, stop=True).then_inc(proj_ready, 1)
                if t < UNITS:
                    a, slot = t // TILES, t % SLOTS
                    pe.wait_ge(q_used, t + 2)
                    pe.wait_ge(keys_in[slot], 16 * HEADS * (t // SLOTS + 1))
                    if t >= 2:
                        pe.wait_ge(shifted, t - 1)
                    for half in range(2):
                        o = scores_ps[:, t % 2, half * 512:half * 512 + 512]
                        if a == 0:
                            nc.tensor.matmul(o, ident_bf[:], mask_bf[:], start=True, stop=False, skip_group_check=True)
                        for b in range(2):
                            mm = nc.tensor.matmul(o[b * SEQ:(b + 1) * SEQ, :], qT[:, t % 2, b * SEQ:(b + 1) * SEQ],
                                                  keys_bd[:, slot, b, half * 512:half * 512 + 512],
                                                  start=(a == 1), stop=True, skip_group_check=True)
                    mm.then_inc(scores_ready, 1)
                if t + 1 < UNITS:
                    q_product(t + 1)
                u = t - 1
                if 0 <= u < UNITS:
                    pe.wait_ge(probs_ready, u + 1)
                    for half in range(2):
                        if u >= 1:
                            pe.wait_ge(probsT_dve if half else probsT_act, u)
                        for j in range(4):
                            hp = half * 4 + j
                            mm = nc.tensor.transpose(probsT_ps[:, half, j * P:(j + 1) * P],
                                                     probs[:, u % 2, hp * P:(hp + 1) * P], ident[:])
                        mm.then_inc(probsT_ready, 1)
                u = t - 2
                if 0 <= u < UNITS:
                    a, tile = u // TILES, u % TILES
                    pe.wait_ge(probsT_act, u + 1)
                    pe.wait_ge(probsT_dve, u + 1)
                    if u >= 1:
                        pe.wait_ge(summed_ready, u)
                    for hp in range(HP):
                        for b in range(2):
                            mm = nc.tensor.matmul(
                                dve_ps[b * SEQ:(b + 1) * SEQ, hp * 2 * VW:(hp + 1) * 2 * VW],
                                probsT[:, u % 2, hp * P + b * SEQ:hp * P + (b + 1) * SEQ],
                                vals[:, a, 2 * tile + b, hp, :, :], start=True, stop=True)
                    mm.then_inc(pv_ready, 1)
                u = t - 3
                if 0 <= u < UNITS:
                    pe.wait_ge(xn_ready, u + 1)
                    if t + 1 < UNITS:
                        pe.wait_ge(q_used, t + 3)
                    elif u >= 1:
                        pe.wait_ge(yT_ready, u)
                    nc.tensor.transpose(act_ps[:, 0:P], xn[:, u % 2, :], ident[:]).then_inc(xnT_ready, 1)
                u = t - 2
                if 0 <= u < UNITS:
                    pe.wait_ge(mixed_ready, u + 1)
                    nc.tensor.transpose(dve_ps[:, 0:P], mixed[:, u % 2, :], ident[:]).then_inc(mixedT_ready, 1)

            pe.wait_ge(yT_ready, UNITS)
            for tile in range(TILES):
                mm = nc.tensor.matmul(dve_ps[:, tile * E:(tile + 1) * E], yT[:, 1, tile * P:(tile + 1) * P], rw_sb[:],
                                      start=True, stop=True)
            mm.then_inc(logits_ready, 1)

            def up(g):
                c, e = g // E, g % E
                pe.wait_ge(w1_in[e], 16)
                for k in range(FC):
                    n = g * FC + k
                    if g >= 1:
                        pe.wait_ge(gelu_ready, n - FC + 1)
                    nc.tensor.matmul(scores_ps[:, k // 2, (k % 2) * 512:(k % 2) * 512 + 512],
                                     w1_sb[:, e, k * P:(k + 1) * P], yT[:, 1, c * CH:(c + 1) * CH],
                                     start=True, stop=True).then_inc(up_ready, 1)

            def down(g):
                e = g % E
                pe.wait_ge(w2_in[e], 16)
                pe.wait_ge(gelu_ready, (g + 1) * FC)
                if g >= 2:
                    pe.wait_ge(acc_ready, (g - 1) * TPC)
                for j in range(TPC):
                    for k in range(FC):
                        mm = nc.tensor.matmul(probsT_ps[:, g % 2, j * D:(j + 1) * D],
                                              h_sb[:, (g % 2) * FC + k, j * P:(j + 1) * P], w2_sb[:, e, k, :],
                                              start=(k == 0), stop=(k == FC - 1))
                mm.then_inc(down_ready, 1)

            for g in range(STEPS + 1):
                if g < STEPS:
                    up(g)
                if g == 1:
                    pe.wait_ge(gate_ready, 1)
                    nc.tensor.transpose(act_ps[0:TILES * E, 128:256], gate[:].rearrange("p t e -> p (t e)"),
                                        ident[:]).then_inc(gateT_ready, 1)
                if g >= 1:
                    down(g - 1)
                if g == 2:
                    pe.wait_ge(gateT_used, 1)
                    pe.wait_ge(b2_in, 16 * TILES)
                    nc.tensor.matmul(act_ps[:, 0:512], gateT[:], b2_bd[:, 0:512], start=True, stop=True)
                    nc.tensor.matmul(dve_ps[:, 0:512], gateT[:], b2_bd[:, 512:1024], start=True, stop=True).then_inc(b2_ready, 1)

        @block.vector
        def _(dve):
            nc.vector.memset(keys_bd[:, 2:4].rearrange("p s b n -> p (s b n)"), 0.0).then_inc(zeroed_v, 1)
            nc.vector.memset(vals[:].rearrange("p a b h r v -> p (a b h r v)"), 0.0).then_inc(zeroed_v, 1)
            dve.wait_ge(zeroed_v, 2)
            for par in range(2):
                nc.vector.memset(vals[par * SEQ:(par + 1) * SEQ, :, :, :, par, HD:VW].rearrange("p a b h v -> p (a b) h v"),
                                 1.0).then_inc(zeroed_v, 1)
            dve.wait_ge(bv_in, 32)
            for n, (what, a, part, who) in enumerate(opening):
                if who != "dve":
                    continue
                dve.wait_ge(pro_ready, n + 1)
                if what == "T":
                    nc.vector.tensor_copy(srcT[:, a, part * 512:part * 512 + 512], open_bank(n)).then_inc(pro_dve, 1)
                else:
                    for par in range(2):
                        r = slice(par * SEQ, (par + 1) * SEQ)
                        for_heads = "p (b h r d) -> p b h r d"
                        src = open_bank(n)[r, :].rearrange(for_heads, b=4, h=HP, r=2)[:, :, :, par, :]
                        bias = bc[f"bv{a}"][r, :].rearrange("p (h r d) -> p h r d", h=HP, r=2)[:, :, par, :]
                        bias = bias.unsqueeze(1).broadcast_to((SEQ, 4, HP, HD))
                        ins = nc.vector.tensor_tensor(vals[r, a, part * 4:part * 4 + 4, :, par, 0:HD], src, bias, ALU.add)
                    ins.then_inc(pro_dve, 1)

            for t in range(UNITS + 4):
                w = t - 3
                if 0 <= w < UNITS:
                    n, tile = w // TILES, w % TILES
                    dve.wait_ge(proj_ready, w + 1)
                    if w == 0:
                        dve.wait_ge(res0_ready, 1)
                    if n == 1:
                        dve.wait_ge(res_ready, tile + 1)
                    nc.vector.tensor_tensor(summed[:, w % 2, :], dve_ps[:, 0:D], res[:, n, tile, :],
                                            ALU.add).then_inc(summed_ready, 1)
                    dve.wait_ge(summed_ready, w + 1)
                    nc.vector.bn_stats(stats[:, w % 2, :], summed[:, w % 2, :]).then_inc(stats_ready, 1)
                    dve.wait_ge(stats_ready, w + 1)
                    nc.vector.bn_aggr(mv[:, w % 2, :], stats[:, w % 2, :]).then_inc(mv_ready, 1)
                    dve.wait_ge(mv_ready, w + 1)
                    nc.vector.tensor_scalar(veps[:, w % 2:w % 2 + 1], mv[:, w % 2, 1:2], EPS, None,
                                            ALU.add).then_inc(veps_ready, 1)
                if t < UNITS:
                    dve.wait_ge(scores_ready, t + 1)
                    nc.vector.tensor_reduce(top[:, t % 2, :], scores_ps[:, t % 2, :].rearrange("p (h k) -> p h k", k=SEQ),
                                            AX.X, ALU.max).then_inc(max_ready, 1)
                if 0 <= w < UNITS:
                    dve.wait_ge(rstd_ready, w + 1)
                    if w >= 2:
                        dve.wait_ge(xnT_ready, w - 1)
                        dve.wait_ge(res_ready, w - 1)
                    nc.vector.tensor_scalar(xn[:, w % 2, :], summed[:, w % 2, :], mv[:, w % 2, 0:1],
                                            rstd[:, w % 2:w % 2 + 1], ALU.subtract, ALU.mult).then_inc(xn_ready, 1)
                if t < UNITS:
                    dve.wait_ge(max_ready, t + 1)
                    if t >= 2:
                        dve.wait_ge(probsT_ready, 2 * (t - 1))
                    nc.vector.tensor_tensor(
                        probs[:, t % 2, :].rearrange("p (h k) -> p h k", k=SEQ),
                        scores_ps[:, t % 2, :].rearrange("p (h k) -> p h k", k=SEQ),
                        top[:, t % 2, :].unsqueeze(2).broadcast_to((P, HEADS, SEQ)), ALU.subtract).then_inc(shifted, 1)
                u = t - 2
                if 0 <= u < UNITS:
                    dve.wait_ge(pv_ready, u + 1)
                    pv = dve_ps[:, 0:HEADS * VW].rearrange("p (h v) -> p h v", v=VW)
                    nc.vector.reciprocal(rsum[:, u % 2, :], pv[:, :, HD]).then_inc(rsum_ready, 1)
                    dve.wait_ge(rsum_ready, u + 1)
                    if u >= 2:
                        dve.wait_ge(mixedT_ready, u - 1)
                    nc.vector.tensor_tensor(mixed[:, u % 2, :].rearrange("p (h v) -> p h v", v=HD), pv[:, :, 0:HD],
                                            rsum[:, u % 2, :].unsqueeze(2).broadcast_to((P, HEADS, HD)),
                                            ALU.mult).then_inc(mixed_ready, 1)
                u = t - 1
                if 0 <= u < UNITS:
                    dve.wait_ge(probsT_ready, 2 * u + 2)
                    if u >= 2:
                        dve.wait_ge(pv_ready, u - 1)
                    nc.vector.tensor_copy(probsT[:, u % 2, 512:1024], probsT_ps[:, 1, :]).then_inc(probsT_dve, 1)

            count = [0]

            def link(ins):
                count[0] += 1
                ins.then_inc(rchain, 1)
                dve.wait_ge(rchain, count[0])

            def over_experts(v):
                return v.unsqueeze(2).broadcast_to((P, TILES, E))

            lg, sh, ex, pr, key, pick1, left, pick2, tmp = (r_buf[:, i] for i in range(9))
            lmax, lsum, m1, dif, e21, den, gate1, gate2 = (r_one[:, i] for i in range(8))
            ranks = rank[:].unsqueeze(1).broadcast_to((P, TILES, E))
            dve.wait_ge(logits_ready, 1)
            link(nc.vector.tensor_tensor(lg, dve_ps[:, 0:TILES * E].rearrange("p (t e) -> p t e", e=E),
                                         rb_bc[:].unsqueeze(1).broadcast_to((P, TILES, E)), ALU.add))
            link(nc.vector.tensor_reduce(lmax, lg, AX.X, ALU.max))
            nc.vector.tensor_tensor(sh, lg, over_experts(lmax), ALU.subtract).then_inc(r_exp_in, 1)
            dve.wait_ge(r_exp, 1)
            link(nc.vector.tensor_reduce(lsum, ex, AX.X, ALU.add))
            link(nc.vector.reciprocal(den, lsum))
            link(nc.vector.tensor_tensor(pr, ex, over_experts(den), ALU.mult))
            link(nc.vector.tensor_reduce(m1, pr, AX.X, ALU.max))

            def pick(src, most, chosen):
                link(nc.vector.tensor_tensor(key, src, over_experts(most), ALU.is_equal))
                link(nc.vector.tensor_tensor(key, key, ranks, ALU.mult))
                link(nc.vector.tensor_reduce(lmax, key, AX.X, ALU.max))
                link(nc.vector.tensor_tensor(chosen, key, over_experts(lmax), ALU.is_equal))

            pick(pr, m1, pick1)
            link(nc.vector.scalar_tensor_tensor(left.rearrange("p t e -> p (t e)"), pick1.rearrange("p t e -> p (t e)"),
                                                -2.0, pr.rearrange("p t e -> p (t e)"), ALU.mult, ALU.add))
            link(nc.vector.tensor_reduce(lsum, left, AX.X, ALU.max))
            nc.vector.tensor_tensor(dif, lsum, m1, ALU.subtract).then_inc(r_exp_in, 1)
            pick(left, lsum, pick2)
            dve.wait_ge(r_exp, 2)
            link(nc.vector.tensor_scalar(den, e21, 1.0, None, ALU.add))
            link(nc.vector.reciprocal(gate1, den))
            link(nc.vector.tensor_tensor(gate2, gate1, e21, ALU.mult))
            link(nc.vector.tensor_tensor(pick1, pick1, over_experts(gate1), ALU.mult))
            link(nc.vector.tensor_tensor(tmp, pick2, over_experts(gate2), ALU.mult))
            nc.vector.tensor_tensor(gate[:], pick1, tmp, ALU.add).then_inc(gate_ready, 1)
            dve.wait_ge(gate_ready, 1)

            def add_expert(g):
                c, e = g // E, g % E
                dve.wait_ge(down_ready, g + 1)
                for j in range(TPC):
                    tile = c * TPC + j
                    if e == 0:
                        nc.vector.tensor_scalar(acc[:, tile, :], probsT_ps[:, g % 2, j * D:(j + 1) * D],
                                                gate[:, tile, e:e + 1], None, ALU.mult).then_inc(acc_ready, 1)
                    else:
                        if j == 0:
                            dve.wait_ge(acc_ready, g * TPC)
                        nc.vector.scalar_tensor_tensor(acc[:, tile, :], probsT_ps[:, g % 2, j * D:(j + 1) * D],
                                                       gate[:, tile, e:e + 1], acc[:, tile, :],
                                                       ALU.mult, ALU.add).then_inc(acc_ready, 1)

            l3 = [0]

            def link3(ins):
                l3[0] += 1
                ins.then_inc(l3chain, 1)

            for g in range(STEPS):
                add_expert(g)
                if g == 1:
                    dve.wait_ge(b2_ready, 1)
                    dve.wait_ge(res_ready, UNITS)
                    for c, bank in enumerate((act_ps, dve_ps)):
                        r = res[:, 2, c * TPC:(c + 1) * TPC, :].rearrange("p t d -> p (t d)")
                        link3(nc.vector.tensor_tensor(r, bank[:, :], r, ALU.add))
                    dve.wait_ge(l3chain, l3[0])
                if g % E == E - 1:
                    c = g // E
                    tiles = range(c * TPC, (c + 1) * TPC)
                    dve.wait_ge(acc_ready, (g + 1) * TPC)
                    s = slice(c * TPC, (c + 1) * TPC)
                    link3(nc.vector.tensor_tensor(acc[:, s, :], acc[:, s, :], res[:, 2, s, :], ALU.add))
                    dve.wait_ge(l3chain, l3[0])
                    for i in tiles:
                        link3(nc.vector.bn_stats(st3[:, i, :], acc[:, i, :]))
                    dve.wait_ge(l3chain, l3[0])
                    for i in tiles:
                        link3(nc.vector.bn_aggr(mv3[:, i, :], st3[:, i, :]))
                    dve.wait_ge(l3chain, l3[0])
                    nc.vector.tensor_scalar(ve3[:, s], mv3[:, s, 1], EPS, None, ALU.add).then_inc(ve3_ready, 1)
                    dve.wait_ge(rstd3_ready, c + 1)
                    for i in tiles:
                        link3(nc.vector.tensor_scalar(acc[:, i, :], acc[:, i, :], mv3[:, i, 0:1], rstd3[:, i:i + 1],
                                                      ALU.subtract, ALU.mult))
                    dve.wait_ge(l3chain, l3[0])
                    link3(nc.vector.tensor_tensor(acc[:, s, :], acc[:, s, :],
                                                  bc["g2"][:].unsqueeze(1).broadcast_to((P, TPC, D)), ALU.mult))
                    dve.wait_ge(l3chain, l3[0])
                    nc.vector.tensor_tensor(y3[:, s, :], acc[:, s, :],
                                            bc["b2"][:].unsqueeze(1).broadcast_to((P, TPC, D)), ALU.add).then_inc(y_ready, 1)

        @block.gpsimd
        def _(pool):
            gc = [0]

            def link(ins):
                gc[0] += 1
                ins.then_inc(chain_g, 1)
                pool.wait_ge(chain_g, gc[0])

            link(nc.gpsimd.memset(ident[:], 0.0))
            nc.gpsimd.affine_select(out=ident[:], in_=ident[:], compare_op=ALU.not_equal, fill=1.0, base=0,
                                    pattern=[[-1, P]], channel_multiplier=1).then_inc(consts, 1)
            for s in range(2):
                nc.gpsimd.memset(keys_bd[:, s].rearrange("p b n -> p (b n)"), 0.0).then_inc(zeroed_g, 1)
            pool.wait_ge(consts, 1)
            nc.gpsimd.tensor_copy(ident_bf[:], ident[:]).then_inc(consts, 1)
            link(nc.gpsimd.memset(mask_bf[:], 0.0))
            for b in range(2):
                m = mask_bf[b * SEQ:(b + 1) * SEQ, :].rearrange("p (h k) -> p h k", k=SEQ)
                ins = nc.gpsimd.affine_select(out=m, in_=m, compare_op=ALU.is_ge, fill=MASKED, base=0,
                                              pattern=[[0, HP], [-1, SEQ]], channel_multiplier=1)
                if b == 0:
                    link(ins)
            ins.then_inc(consts, 1)
            pool.wait_ge(consts, 3)
            nc.gpsimd.memset(neg_half[:], -0.5).then_inc(consts, 1)
            for e in range(E):
                link(nc.gpsimd.memset(rank[:, e:e + 1], float(E - e)))
            link(nc.gpsimd.memset(b2_bd[:], 0.0))
            for i in range(TILES):
                pool.dma_start(b2_bd[i * E:(i + 1) * E, i * D:(i + 1) * D], b2).then_inc(b2_in, 16)
            pool.wait_ge(x_in, 32)
            pool.wait_ge(small_in, 16 * 12)
            nc.gpsimd.tensor_tensor(res[:, 0], x_sb[:], bc["bo0"][:].unsqueeze(1).broadcast_to((P, TILES, D)),
                                    ALU.add).then_inc(res0_ready, 1)
            link(nc.gpsimd.tensor_tensor(b0bo1[:], bc["b0"][:], bc["bo1"][:], ALU.add))
            pool.wait_ge(consts, 4)
            for u in range(UNITS):
                n, tile = u // TILES, u % TILES
                pool.wait_ge(veps_ready, u + 1)
                nc.gpsimd.tensor_tensor(rstd[:, u % 2:u % 2 + 1], veps[:, u % 2:u % 2 + 1], neg_half[:, 0:1],
                                        ALU.pow).then_inc(rstd_ready, 1)
                pool.wait_ge(xn_ready, u + 1)
                nc.gpsimd.tensor_tensor(gx[:], xn[:, u % 2, :], bc[f"g{n}"][:], ALU.mult).then_inc(gx_ready, 1)
                pool.wait_ge(gx_ready, u + 1)
                nc.gpsimd.tensor_tensor(res[:, n + 1, tile, :], gx[:], (b0bo1 if n == 0 else bc["b1"])[:],
                                        ALU.add).then_inc(res_ready, 1)
            for c in range(CHUNKS):
                s = slice(c * TPC, (c + 1) * TPC)
                pool.wait_ge(ve3_ready, c + 1)
                nc.gpsimd.tensor_tensor(rstd3[:, s], ve3[:, s], neg_half[:, 0:TPC], ALU.pow).then_inc(rstd3_ready, 1)


_NAMES = ["x", "ctx_1024"] + [
    "L0_xattn_" + n for n in (
        "sa_wq sa_bq sa_wk sa_bk sa_wv sa_bv sa_wo sa_bo ca_wq ca_bq ca_wk ca_bk ca_wv ca_bv ca_wo ca_bo "
        "ln1_g ln1_b ln2_g ln2_b ln3_g ln3_b router_w router_b e_w1 e_b1 e_w2 e_b2").split()]


def kernel(**inputs):
    import numpy as np
    import concourse.bacc as bacc
    from concourse.bass_utils import run_bass_kernel_spmd

    nc = bacc.Bacc("TRN2", target_bir_lowering=False, num_devices=1)
    arrays, ap = {}, {}
    for name in _NAMES:
        a = np.ascontiguousarray(inputs[name])
        arrays[f"in_{name}"] = a
        ap[name.replace("L0_xattn_", "")] = nc.dram_tensor(
            f"in_{name}", a.shape, mybir.dt.from_np(a.dtype), kind="ExternalInput").ap()
    shape = inputs["x"].shape
    out = nc.dram_tensor("out_0", shape, F32, kind="ExternalOutput").ap()
    att = [{n: ap[f"{a}_{n}"] for n in ("wq", "bq", "wk", "bk", "wv", "bv", "wo", "bo")} for a in ("sa", "ca")]
    build_decoder_layer(nc, ap["x"], ap["ctx_1024"], att[0], att[1],
                        [(ap[f"ln{i}_g"], ap[f"ln{i}_b"]) for i in (1, 2, 3)],
                        ap["router_w"], ap["router_b"], ap["e_w1"], ap["e_b1"], ap["e_w2"], ap["e_b2"], out)
    r = run_bass_kernel_spmd(nc, [arrays], core_ids=[0])
    return r.results[0]["out_0"]
```

```python
from contextlib import ExitStack

import concourse.bass as bass
from concourse import mybir

F32 = mybir.dt.float32
F32R = mybir.dt.float32r
BF16 = mybir.dt.bfloat16
ALU = mybir.AluOpType
ACT = mybir.ActivationFunctionType
AX = mybir.AxisListType

P = 128
D = 128
SEQ = 64
HEADS = 16
HD = D // HEADS
EPS = 1e-5
MASKED = -1e30


def build_decoder_layer(nc, x, ctx, sa, ca, ln, router_w, router_b, w1, b1, w2, b2, out):
    NSEQ = x.shape[0]
    TILES = NSEQ * SEQ // P
    UNITS = 2 * TILES
    E, _, FF = w1.shape
    FC = FF // P
    CH = 512
    CHUNKS = TILES * P // CH
    TPC = CH // P
    STEPS = CHUNKS * E
    SCALE = float(HD) ** -0.5
    HP = HEADS // 2
    SW = HEADS * SEQ
    SETW = 2 * TPC * SW
    LAST = UNITS + 4

    x_tok = x.rearrange("(t b) s d -> (b s) t d", b=2)
    ctx_tok = ctx.rearrange("(t b) s d -> (b s) t d", b=2)
    out_tok = out.rearrange("(t b) s d -> (b s) t d", b=2)
    w1_v = w1.rearrange("e d f -> d e f")
    w2_v = w2.rearrange("e (k p) d -> p e k d", p=P)
    att = [sa, ca]

    with ExitStack() as stack:
        def sb(name, shape, dt=F32):
            return stack.enter_context(nc.sbuf_tensor(name, shape, dt))

        def ps(name, shape):
            return stack.enter_context(nc.psum_tensor(name, shape, F32))

        def sem(name):
            return stack.enter_context(nc.semaphore(name))

        scores_ps = ps("scores_ps", [P, 2, 2, 512])
        probsT_ps = ps("probsT_ps", [P, 2, 512])
        act_ps = ps("act_ps", [P, 512])
        dve_ps = ps("dve_ps", [P, 512])
        LOGITS = 256

        x_sb = sb("x_sb", [P, TILES, D])
        srcT = sb("srcT", [P, 2, TILES * P])
        keysT = sb("keysT", [P, 2, NSEQ, SEQ])
        spread = sb("spread", [P, 2, SETW])
        keys_bd = spread[:].rearrange("p s (b h k) -> p s b h k", h=HEADS, k=SEQ)
        w2_sb = spread[:, 0, 0:E * FC * D].rearrange("p (e k d) -> p e k d", e=E, k=FC)
        W2END = E * FC * D
        r_buf = spread[:, 0, W2END:W2END + 9 * TILES * E].rearrange("p (n t e) -> p n t e", n=9, t=TILES)
        REND = W2END + 9 * TILES * E
        gateT = spread[0:TILES * E, 0, REND:REND + P]
        HB = 2 * FC * CH
        h_sb = spread[:, 1, 0:HB].rearrange("p (n t) -> p n t", n=2 * FC)
        acc = spread[:, 1, HB:HB + TILES * D].rearrange("p (t d) -> p t d", t=TILES)
        y3 = spread[:, 1, HB + TILES * D:HB + 2 * TILES * D].rearrange("p (t d) -> p t d", t=TILES)
        VW = 4 * HD + 2
        vals = sb("vals", [P, 2, TILES, HP, VW])
        wqkvo = {(a, n): sb(f"w{n}{a}", [D, D]) for a in range(2) for n in "qkvo"}
        b1_rows = sb("b1_rows", [E * FC, D])
        b1_cols = sb("b1_cols", [P, E * FC])
        col = {n: sb(f"col_{n}", [D, 1]) for n in ["bq0", "bk0", "bq1", "bk1", "g0", "b0", "g1", "b1"]}
        bc = {n: sb(f"bc_{n}", [P, D]) for n in ["bv0", "bv1", "bo0", "bo1", "g0", "b0", "g1", "b1", "g2", "b2"]}
        rb_bc = sb("rb_bc", [P, E])
        rw_sb = sb("rw_sb", [D, E])
        b2_bd = sb("b2_bd", [TILES * E, TILES * D])
        ident = sb("ident", [P, P])
        ident_bf = sb("ident_bf", [P, P], BF16)
        mask_bf = sb("mask_bf", [P, 512], BF16)
        own_head = sb("own_head", [P, HEADS])
        neg_half = sb("neg_half", [P, TILES])
        rank = sb("rank", [P, E])
        w1_raw = sb("w1_raw", [D, 2, FF])
        w1_hi = sb("w1_hi", [D, E, FF], F32R)
        w1_lo = sb("w1_lo", [D, E, FF], F32R)
        y2T_hi = sb("y2T_hi", [P, TILES * P], F32R)
        y2T_lo = sb("y2T_lo", [P, TILES * P], F32R)

        qT = sb("qT", [P, 2, P])
        top = sb("top", [P, 2, HEADS])
        probs = sb("probs", [P, 2, SW])
        probsT = sb("probsT", [P, 2, SW])
        weighed = sb("weighed", [P, 2, 512])
        rsum = sb("rsum", [P, 2, HEADS])
        mixed = sb("mixed", [P, 2, D])
        mixedT = sb("mixedT", [P, 2, P])
        summed = sb("summed", [P, 2, D])
        stats = sb("stats", [P, 2, 6])
        mv = sb("mv", [P, 2, 2])
        veps = sb("veps", [P, 2])
        rstd = sb("rstd", [P, 2])
        xn = sb("xn", [P, 2, D])
        gx = sb("gx", [P, D])
        res = sb("res", [P, 3, TILES, D])
        ctx_sb = res[:, 2]
        yT = sb("yT", [P, 2, TILES * P])
        r_one = sb("r_one", [P, 8, TILES])
        gate = sb("gate", [P, TILES, E])
        st3 = sb("st3", [P, TILES, 6])
        mv3 = sb("mv3", [P, TILES, 2])
        ve3 = sb("ve3", [P, TILES])
        rstd3 = sb("rstd3", [P, TILES])

        src_in = [[sem(f"src_in{a}{i}") for i in range(2)] for a in range(2)]
        w_in = {k: sem(f"w_in_{k[1]}{k[0]}") for k in wqkvo}
        col_in = {k: sem(f"col_in_{k}") for k in col if k[0:2] in ("bq", "bk")}
        bv_in = [sem(f"bv_in{a}") for a in range(2)]
        lnp_in, bo0_in, b1_in, b2_in, small_in, b1_done = (
            sem("lnp_in"), sem("bo0_in"), sem("b1_in"), sem("b2_in"), sem("small_in"), sem("b1_done"))
        b1T_ready = sem("b1T_ready")
        keys_in = [sem(f"keys_in{s}") for s in range(4)]
        w1_in = [sem(f"w1_in{e}") for e in range(E)]
        w2_in = [sem(f"w2_in{e}") for e in range(E)]
        zeroed, vals_zeroed = sem("zeroed"), [sem(f"vals_zeroed{a}") for a in range(2)]
        consts = sem("consts")
        pro_ready, pro_act, pro_dve = sem("pro_ready"), sem("pro_act"), sem("pro_dve")
        spread_act, spread_dve = sem("spread_act"), sem("spread_dve")
        q_ready, q_used = sem("q_ready"), sem("q_used")
        scores_ready, max_ready, shifted = sem("scores_ready"), sem("max_ready"), sem("shifted")
        probs_ready, probsT_ready, probsT_copied = sem("probs_ready"), sem("probsT_ready"), sem("probsT_copied")
        pv_ready, weighed_ready, weighedT_ready = sem("pv_ready"), sem("weighed_ready"), sem("weighedT_ready")
        rsum_ready, mixed_ready = sem("rsum_ready"), sem("mixed_ready")
        mixedT_ready, mixedT_used = sem("mixedT_ready"), sem("mixedT_used")
        proj_ready, summed_ready, stats_ready = sem("proj_ready"), sem("summed_ready"), sem("stats_ready")
        mv_ready, veps_ready, rstd_ready = sem("mv_ready"), sem("veps_ready"), sem("rstd_ready")
        xn_ready, xnT_ready, yT_ready = sem("xn_ready"), sem("xnT_ready"), sem("yT_ready")
        res0_ready, gx_ready, res_ready = sem("res0_ready"), sem("gx_ready"), sem("res_ready")
        w1_hi_ready, w1_lo_ready = sem("w1_hi_ready"), sem("w1_lo_ready")
        y2T_hi_ready, y2T_lo_ready = sem("y2T_hi_ready"), sem("y2T_lo_ready")
        logits_ready, rchain, r_exp_in, r_exp = sem("logits_ready"), sem("rchain"), sem("r_exp_in"), sem("r_exp")
        gate_ready, gateT_ready, gateT_used, b2_ready = sem("gate_ready"), sem("gateT_ready"), sem("gateT_used"), sem("b2_ready")
        up_ready, gelu_ready, down_ready, acc_ready = sem("up_ready"), sem("gelu_ready"), sem("down_ready"), sem("acc_ready")
        l3chain, ve3_ready, rstd3_ready, y_ready, stored = (
            sem("l3chain"), sem("ve3_ready"), sem("rstd3_ready"), sem("y_ready"), sem("stored"))
        chain_g = sem("chain_g")

        side = [("T", 0, 0, "dve", None), ("T", 0, 1, "act", None), ("K", 0, 0, "act", None),
                ("K", 0, 1, "act", None), ("V", 0, 0, "dve", None), ("V", 0, 1, "dve", None),
                ("V", 0, 2, "dve", 0), ("V", 0, 3, "dve", 1), ("T", 1, 0, "act", 2), ("T", 1, 1, "act", 3),
                ("K", 1, 0, "act", 4), ("K", 1, 1, "act", 5)] + [("V", 1, g, "dve", 6 + g) for g in range(4)]
        OPENING = [n for n, o in enumerate(side) if o[4] is None]

        def side_bank(n):
            if side[n][4] is not None:
                return scores_ps[:, (side[n][4] + 1) % 2, 0, :]
            return scores_ps[:, n // 2, n % 2, :] if n < 4 else probsT_ps[:, n - 4, :]

        def read_count(n):
            who = side[n][3]
            return (pro_act if who == "act" else pro_dve), sum(o[3] == who for o in side[:n + 1])

        def product(what, a, part):
            return next(n for n, o in enumerate(side) if o[:3] == (what, a, part))

        def side_of(rnd):
            return next((n for n, o in enumerate(side) if o[4] == rnd), None)

        B1_ROUND = TILES + 4
        ACT_HEADS = 6

        block = stack.enter_context(nc.Block())

        @block.sync
        def _(sp):
            half = TILES // 2

            def column(n, v):
                return sp.dma_start(col[n][:], v.rearrange("(d a) -> d a", a=1))

            def load_w(a, n):
                sp.dma_start(wqkvo[a, n][:], att[a]["w" + n]).then_inc(w_in[a, n], 16)

            def load_src(a, i):
                dst, src = ((x_sb, x_tok), (ctx_sb, ctx_tok))[a]
                sp.dma_start(dst[:, i * half:(i + 1) * half, :], src[:, i * half:(i + 1) * half, :]).then_inc(src_in[a][i], 16)

            load_src(0, 0)
            load_w(0, "k")
            load_src(0, 1)
            column("bk0", sa["bk"]).then_inc(col_in["bk0"], 16)
            load_w(0, "q")
            column("bq0", sa["bq"]).then_inc(col_in["bq0"], 16)
            load_w(0, "v")
            sp.dma_start(bc["bv0"][:], sa["bv"].partition_broadcast(P)).then_inc(bv_in[0], 16)
            load_w(0, "o")
            sp.dma_start(bc["bo0"][:], sa["bo"].partition_broadcast(P)).then_inc(bo0_in, 16)

            def load_w1(e):
                if e >= 2:
                    sp.wait_ge(w1_lo_ready, e - 1)
                sp.dma_start(w1_raw[:, e % 2, :], w1_v[:, e, :]).then_inc(w1_in[e], 16)

            def spread_keys(s):
                a, part = s // 2, s % 2
                sem_, v = read_count(product("K", a, part))
                sp.wait_ge(sem_, v)
                sp.wait_ge(zeroed, 1)
                if s >= 2:
                    sp.wait_ge(scores_ready, (s - 1) * TPC)
                for h in range(HEADS):
                    r = slice(h * HD, (h + 1) * HD)
                    sp.dma_start(keys_bd[r, s % 2, :, h, :], keysT[r, a, part * 8:part * 8 + 8, :]).then_inc(keys_in[s], 16)

            spread_keys(1)
            for n in range(2):
                column(f"g{n}", ln[n][0]).then_inc(lnp_in, 16)
                column(f"b{n}", ln[n][1]).then_inc(lnp_in, 16)
                sp.dma_start(bc[f"g{n}"][:], ln[n][0].partition_broadcast(P)).then_inc(lnp_in, 16)
                sp.dma_start(bc[f"b{n}"][:], ln[n][1].partition_broadcast(P)).then_inc(lnp_in, 16)
            sp.dma_start(bc["bo1"][:], ca["bo"].partition_broadcast(P)).then_inc(lnp_in, 16)
            load_src(1, 0)
            load_src(1, 1)
            load_w(1, "k")
            column("bk1", ca["bk"]).then_inc(col_in["bk1"], 16)
            load_w1(0)
            load_w1(1)
            load_w(1, "v")
            sp.dma_start(bc["bv1"][:], ca["bv"].partition_broadcast(P)).then_inc(bv_in[1], 16)
            load_w(1, "q")
            column("bq1", ca["bq"]).then_inc(col_in["bq1"], 16)
            load_w(1, "o")
            load_w1(2)
            load_w1(3)
            spread_keys(2)
            load_w1(4)
            load_w1(5)
            load_w1(6)
            load_w1(7)
            spread_keys(3)
            for e in range(E):
                if e == 0:
                    sp.wait_ge(scores_ready, 3 * TPC)
                sp.dma_start(w2_sb[:, e, :, :], w2_v[:, e, :, :]).then_inc(w2_in[e], 16)
            for c in range(CHUNKS):
                sp.wait_ge(y_ready, c + 1)
                sp.dma_start(out_tok[:, c * TPC:(c + 1) * TPC, :], y3[:, c * TPC:(c + 1) * TPC, :]).then_inc(stored, 16)
            sp.wait_ge(stored, 16 * CHUNKS)

        @block.scalar
        def _(act):
            def side_read(n):
                what, a, part, who, _ = side[n]
                if who != "act":
                    return
                act.wait_ge(pro_ready, n + 1)
                if what == "T":
                    nc.scalar.copy(srcT[:, a, part * 512:part * 512 + 512], side_bank(n)).then_inc(pro_act, 1)
                else:
                    act.wait_ge(col_in[f"bk{a}"], 16)
                    nc.scalar.activation(
                        keysT[:, a, part * 8:part * 8 + 8, :], side_bank(n).rearrange("p (b k) -> p b k", k=SEQ),
                        ACT.Identity, bias=col[f"bk{a}"][:]).then_inc(pro_act, 1)

            def q_copy(u):
                a = u // TILES
                act.wait_ge(q_ready, u + 1)
                act.wait_ge(col_in[f"bq{a}"], 16)
                if u >= 2:
                    act.wait_ge(scores_ready, u - 1)
                nc.scalar.activation(qT[:, u % 2, :], act_ps[:, 0:P], ACT.Identity,
                                     bias=col[f"bq{a}"][:]).then_inc(q_used, 1)

            side_read(1)
            side_read(2)
            q_copy(0)
            act.wait_ge(pro_act, 2)
            act.wait_ge(consts, 1)
            for h in range(ACT_HEADS):
                nc.scalar.activation(keys_bd[:, 0, :, h, :], keysT[:, 0, 0:8, :], ACT.Copy,
                                     scale=own_head[:, h:h + 1]).then_inc(spread_act, 1)
            side_read(3)
            def mixedT_copy(t):
                u = t - 3
                if 0 <= u < UNITS:
                    act.wait_ge(mixedT_ready, u + 1)
                    if u >= 2:
                        act.wait_ge(proj_ready, u - 1)
                    nc.scalar.copy(mixedT[:, u % 2, :], act_ps[:, 0:P]).then_inc(mixedT_used, 1)

            def yT_copy(t):
                u = t - 4
                if u >= 0:
                    n, tile = u // TILES, u % TILES
                    act.wait_ge(xnT_ready, u + 1)
                    if u == 0:
                        act.wait_ge(lnp_in, 16 * 9)
                    nc.scalar.activation(yT[:, n, tile * P:(tile + 1) * P], act_ps[:, 0:P], ACT.Identity,
                                         bias=col[f"b{n}"][:], scale=col[f"g{n}"][:]).then_inc(yT_ready, 1)

            def weighed_copy(t):
                u = t - 2
                if 0 <= u < UNITS:
                    act.wait_ge(pv_ready, u + 1)
                    if u >= 2:
                        act.wait_ge(weighedT_ready, u - 1)
                    nc.scalar.copy(weighed[:, u % 2, :], scores_ps[:, (t + 1) % 2, 1, :]).then_inc(weighed_ready, 1)

            def queries(t):
                if t + 1 < UNITS:
                    q_copy(t + 1)
                if t == B1_ROUND:
                    act.wait_ge(b1T_ready, 1)
                    nc.scalar.copy(b1_cols[:], act_ps[:, 128:128 + E * FC]).then_inc(b1_done, 1)

            def probsT_copy(t):
                u = t - 1
                if 0 <= u < UNITS:
                    if u >= 2:
                        act.wait_ge(pv_ready, u - 1)
                    for half in range(2):
                        act.wait_ge(probsT_ready, 2 * u + half + 1)
                        nc.scalar.copy(probsT[:, u % 2, half * 512:half * 512 + 512],
                                       probsT_ps[:, half, :]).then_inc(probsT_copied, 1)

            def side_stage(t):
                if side_of(t) is not None:
                    side_read(side_of(t))

            def exponentials(t):
                if t < UNITS:
                    act.wait_ge(shifted, t + 1)
                    nc.scalar.activation(probs[:, t % 2, :], probs[:, t % 2, :], ACT.Exp,
                                         scale=SCALE).then_inc(probs_ready, 1)

            def w1_leading(t):
                e = t - 2
                if 0 <= e < E:
                    act.wait_ge(w1_in[e], 16)
                    nc.scalar.copy(w1_hi[:, e, :], w1_raw[:, e % 2, :]).then_inc(w1_hi_ready, 1)

            for t in range(LAST):
                mixedT_copy(t)
                yT_copy(t)
                weighed_copy(t)
                queries(t)
                probsT_copy(t)
                side_stage(t)
                exponentials(t)
                w1_leading(t)

            act.wait_ge(r_exp_in, 1)
            nc.scalar.activation(r_buf[:, 2], r_buf[:, 1], ACT.Exp).then_inc(r_exp, 1)
            act.wait_ge(r_exp_in, 2)
            nc.scalar.activation(r_one[:, 4], r_one[:, 3], ACT.Exp).then_inc(r_exp, 1)

            def gelus(g):
                e = g % E
                for k in range(FC):
                    n = g * FC + k
                    act.wait_ge(up_ready, n + 1)
                    if g >= 2:
                        act.wait_ge(down_ready, g - 1)
                    nc.scalar.activation(h_sb[:, n % (2 * FC), :], scores_ps[:, k // 2, k % 2, :],
                                         ACT.Gelu, bias=b1_cols[:, e * FC + k:e * FC + k + 1]).then_inc(gelu_ready, 1)

            for g in range(STEPS):
                gelus(g)
                if g == 1:
                    act.wait_ge(gateT_ready, 1)
                    nc.scalar.copy(gateT, act_ps[0:TILES * E, 128:256]).then_inc(gateT_used, 1)

        @block.tensor
        def _(pe):
            src_sb = [x_sb, ctx_sb]

            def side_product(n):
                what, a, part, who, rnd = side[n]
                bank = side_bank(n)
                if what == "T":
                    pe.wait_ge(src_in[a][part], 16)
                    for j in range(4):
                        mm = nc.tensor.transpose(bank[:, j * P:(j + 1) * P], src_sb[a][:, part * 4 + j, :], ident[:])
                elif what == "K":
                    s, v = read_count(product("T", a, part))
                    pe.wait_ge(s, v)
                    pe.wait_ge(w_in[a, "k"], 16)
                    mm = nc.tensor.matmul(bank, wqkvo[a, "k"][:], srcT[:, a, part * 512:part * 512 + 512],
                                          start=True, stop=True)
                else:
                    s, v = read_count(product("T", a, part // 2))
                    pe.wait_ge(s, v)
                    pe.wait_ge(w_in[a, "v"], 16)
                    for j in range(4):
                        b = part * 4 + j
                        for r in range(2):
                            mm = nc.tensor.matmul(bank[r * SEQ:(r + 1) * SEQ, j * D:(j + 1) * D],
                                                  srcT[:, a, b * SEQ:(b + 1) * SEQ], wqkvo[a, "v"][:],
                                                  start=True, stop=True)
                mm.then_inc(pro_ready, 1)

            def q_product(u):
                a, tile = u // TILES, u % TILES
                pe.wait_ge(w_in[a, "q"], 16)
                if a == 0:
                    rhs = srcT[:, 0, tile * P:(tile + 1) * P]
                    if tile % TPC == 0:
                        s, v = read_count(product("T", 0, tile // TPC))
                        pe.wait_ge(s, v)
                else:
                    pe.wait_ge(yT_ready, tile + 1)
                    rhs = yT[:, 0, tile * P:(tile + 1) * P]
                nc.tensor.matmul(act_ps[:, 0:P], wqkvo[a, "q"][:], rhs, start=True, stop=True).then_inc(q_ready, 1)

            pe.wait_ge(consts, 2)
            for n in OPENING[:3]:
                side_product(n)
            q_product(0)
            for n in OPENING[3:]:
                side_product(n)
            pe.wait_ge(consts, 4)
            def scores(t, half):
                if t >= UNITS:
                    return
                slot = t % 2
                a, s = t // TILES, t // TPC
                if half == 0:
                    pe.wait_ge(q_used, t + 1)
                    if s == 0:
                        pe.wait_ge(spread_act, ACT_HEADS)
                        pe.wait_ge(spread_dve, HEADS - ACT_HEADS)
                    else:
                        pe.wait_ge(keys_in[s], 16 * HEADS)
                    if t < 2:
                        for n in OPENING[2 * t:2 * t + 2]:
                            pe.wait_ge(*read_count(n))
                    else:
                        pe.wait_ge(shifted, t - 1)
                        if t >= 3:
                            pe.wait_ge(weighed_ready, t - 2)
                    if side_of(t - 1) is not None:
                        pe.wait_ge(*read_count(side_of(t - 1)))
                o = scores_ps[:, slot, half, :]
                if a == 0:
                    nc.tensor.matmul(o, ident_bf[:], mask_bf[:], start=True, stop=False, skip_group_check=True)
                for b in range(2):
                    mm = nc.tensor.matmul(
                        o[b * SEQ:(b + 1) * SEQ, :], qT[:, slot, b * SEQ:(b + 1) * SEQ],
                        keys_bd[:, s % 2, 2 * (t % TPC) + b, half * HP:(half + 1) * HP, :],
                        start=(a == 1), stop=True, skip_group_check=True)
                if half == 1:
                    mm.then_inc(scores_ready, 1)

            def mixed_transpose(t):
                u, w = t - 4, t - 3
                if 0 <= w < UNITS:
                    pe.wait_ge(mixed_ready, w + 1)
                    if u - 1 >= 0:
                        pe.wait_ge(yT_ready, u)
                    nc.tensor.transpose(act_ps[:, 0:P], mixed[:, w % 2, :], ident[:]).then_inc(mixedT_ready, 1)

            def project(t):
                w = t - 3
                if 0 <= w < UNITS:
                    pe.wait_ge(mixedT_used, w + 1)
                    pe.wait_ge(w_in[w // TILES, "o"], 16)
                    nc.tensor.matmul(dve_ps[:, 0:D], mixedT[:, w % 2, :], wqkvo[w // TILES, "o"][:],
                                     start=True, stop=True).then_inc(proj_ready, 1)

            def xn_transpose(t):
                u = t - 4
                if u >= 0:
                    pe.wait_ge(xn_ready, u + 1)
                    nc.tensor.transpose(act_ps[:, 0:P], xn[:, u % 2, :], ident[:]).then_inc(xnT_ready, 1)

            def side_stage(t):
                if side_of(t) is not None:
                    if t >= 1:
                        pe.wait_ge(shifted, t)
                    else:
                        for n in OPENING[2:4]:
                            pe.wait_ge(*read_count(n))
                    side_product(side_of(t))

            def weigh(t):
                v, other = t - 2, (t + 1) % 2
                if 0 <= v < UNITS:
                    a, tile = v // TILES, v % TILES
                    pe.wait_ge(probsT_copied, 2 * v + 2)
                    pe.wait_ge(pro_dve, read_count(product("V", a, tile // 2))[1])
                    pe.wait_ge(shifted, min(t, UNITS))
                    for hp in range(HP):
                        r = (hp % 2) * SEQ
                        mm = nc.tensor.matmul(
                            scores_ps[r:r + VW, other, 1, (hp // 2) * P:(hp // 2 + 1) * P],
                            vals[:, a, tile, hp, :], probsT[:, v % 2, hp * P:(hp + 1) * P], start=True, stop=True)
                    mm.then_inc(pv_ready, 1)

            def queries(t):
                u, w = t - 4, t - 3
                if t + 1 < UNITS:
                    if u >= 0:
                        pe.wait_ge(yT_ready, u + 1)
                    elif w >= 0:
                        pe.wait_ge(mixedT_used, w + 1)
                    if t == B1_ROUND:
                        pe.wait_ge(b1_in, 16)
                        nc.tensor.transpose(act_ps[:, 128:128 + E * FC], b1_rows[:],
                                            ident[0:E * FC, 0:E * FC]).then_inc(b1T_ready, 1)
                    q_product(t + 1)

            def probs_transpose(t):
                p = t - 1
                if 0 <= p < UNITS:
                    pe.wait_ge(probs_ready, p + 1)
                    for half in range(2):
                        if p >= 1:
                            pe.wait_ge(probsT_copied, 2 * p - 1 + half)
                        else:
                            pe.wait_ge(*read_count(OPENING[4 + half]))
                        for j in range(4):
                            hp = half * 4 + j
                            mm = nc.tensor.transpose(probsT_ps[:, half, j * P:(j + 1) * P],
                                                     probs[:, p % 2, hp * P:(hp + 1) * P], ident[:])
                        mm.then_inc(probsT_ready, 1)

            def logits(t):
                u = t - 4
                if u >= TILES:
                    tile = u % TILES
                    if u == TILES:
                        pe.wait_ge(small_in, 16 * 4)
                        pe.wait_ge(b1_done, 1)
                    pe.wait_ge(yT_ready, u + 1)
                    if t + 1 < UNITS:
                        pe.wait_ge(q_used, t + 2)
                    mm = nc.tensor.matmul(act_ps[:, LOGITS + tile * E:LOGITS + (tile + 1) * E],
                                          yT[:, 1, tile * P:(tile + 1) * P], rw_sb[:], start=True, stop=True)
                    if tile == TILES - 1:
                        mm.then_inc(logits_ready, 1)

            def weighed_transpose(t):
                v, w = t - 2, t - 3
                if 0 <= v < UNITS:
                    pe.wait_ge(weighed_ready, v + 1)
                    if w >= 0:
                        pe.wait_ge(summed_ready, w + 1)
                    for r in range(4):
                        mm = nc.tensor.transpose(dve_ps[:, r * P:(r + 1) * P], weighed[:, v % 2, r * P:(r + 1) * P], ident[:])
                    mm.then_inc(weighedT_ready, 1)

            for t in range(LAST):
                scores(t, 0)
                mixed_transpose(t)
                scores(t, 1)
                project(t)
                xn_transpose(t)
                side_stage(t)
                weigh(t)
                queries(t)
                probs_transpose(t)
                logits(t)
                weighed_transpose(t)

            def up(g):
                c, e = g // E, g % E
                pe.wait_ge(w1_lo_ready, e + 1)
                pe.wait_ge(y2T_lo_ready, (c + 1) * TPC)
                for k in range(FC):
                    n = g * FC + k
                    if g >= 1:
                        pe.wait_ge(gelu_ready, n - FC + 1)
                    o = scores_ps[:, k // 2, k % 2, :]
                    f = slice(k * P, (k + 1) * P)
                    tok = slice(c * CH, (c + 1) * CH)
                    nc.tensor.matmul(o, w1_hi[:, e, f], y2T_hi[:, tok], start=True, stop=False)
                    nc.tensor.matmul(o, w1_hi[:, e, f], y2T_lo[:, tok], start=False, stop=False)
                    nc.tensor.matmul(o, w1_lo[:, e, f], y2T_hi[:, tok], start=False, stop=True).then_inc(up_ready, 1)

            def down(g):
                e = g % E
                pe.wait_ge(w2_in[e], 16)
                pe.wait_ge(gelu_ready, (g + 1) * FC)
                if g >= 2:
                    pe.wait_ge(acc_ready, (g - 1) * TPC)
                for j in range(TPC):
                    for k in range(FC):
                        mm = nc.tensor.matmul(probsT_ps[:, g % 2, j * D:(j + 1) * D],
                                              h_sb[:, (g % 2) * FC + k, j * P:(j + 1) * P], w2_sb[:, e, k, :],
                                              start=(k == 0), stop=(k == FC - 1))
                mm.then_inc(down_ready, 1)

            for g in range(STEPS + 1):
                if g < STEPS:
                    up(g)
                if g == 1:
                    pe.wait_ge(gate_ready, 1)
                    nc.tensor.transpose(act_ps[0:TILES * E, 128:256], gate[:].rearrange("p t e -> p (t e)"),
                                        ident[:]).then_inc(gateT_ready, 1)
                if g >= 1:
                    down(g - 1)
                if g == 2:
                    pe.wait_ge(gateT_used, 1)
                    pe.wait_ge(b2_in, 16 * TILES)
                    nc.tensor.matmul(act_ps[:, 0:512], gateT, b2_bd[:, 0:512], start=True, stop=True)
                    nc.tensor.matmul(dve_ps[:, 0:512], gateT, b2_bd[:, 512:1024], start=True, stop=True).then_inc(b2_ready, 1)

        @block.vector
        def _(dve):
            def side_read(n):
                what, a, part, who, _ = side[n]
                if who != "dve":
                    return
                dve.wait_ge(pro_ready, n + 1)
                if what == "T":
                    nc.vector.tensor_copy(srcT[:, a, part * 512:part * 512 + 512], side_bank(n)).then_inc(pro_dve, 1)
                    return
                dve.wait_ge(bv_in[a], 16)
                dve.wait_ge(vals_zeroed[a], 3)
                for par in range(2):
                    r = slice(par * SEQ, (par + 1) * SEQ)
                    for b in range(2):
                        src = side_bank(n)[r, :].rearrange("p (t b h r d) -> p t b h r d", t=2, b=2, h=HP, r=2)[:, :, b, :, par, :]
                        bias = bc[f"bv{a}"][r, :].rearrange("p (h r d) -> p h r d", h=HP, r=2)[:, :, par, :]
                        bias = bias.unsqueeze(1).broadcast_to((SEQ, 2, HP, HD))
                        c = (b * 2 + par) * HD
                        ins = nc.vector.tensor_tensor(vals[r, a, part * 2:part * 2 + 2, :, c:c + HD], src, bias, ALU.add)
                ins.then_inc(pro_dve, 1)

            def zero_vals(a):
                nc.vector.memset(vals[:, a].rearrange("p t h v -> p (t h v)"), 0.0).then_inc(vals_zeroed[a], 1)
                dve.wait_ge(vals_zeroed[a], 1)
                for par in range(2):
                    nc.vector.memset(vals[par * SEQ:(par + 1) * SEQ, a, :, :, 4 * HD + par], 1.0).then_inc(vals_zeroed[a], 1)

            zero_vals(0)
            side_read(0)
            dve.wait_ge(pro_act, 2)
            dve.wait_ge(consts, 1)
            for h in range(ACT_HEADS, HEADS):
                nc.vector.tensor_scalar(keys_bd[:, 0, :, h, :], keysT[:, 0, 0:8, :], own_head[:, h:h + 1], None,
                                        ALU.mult).then_inc(spread_dve, 1)
            side_read(4)
            side_read(5)

            def residual(t):
                w = t - 3
                if 0 <= w < UNITS:
                    n, tile = w // TILES, w % TILES
                    dve.wait_ge(proj_ready, w + 1)
                    if w == 0:
                        dve.wait_ge(res0_ready, 1)
                    if n == 1:
                        dve.wait_ge(res_ready, tile + 1)
                    nc.vector.tensor_tensor(summed[:, w % 2, :], dve_ps[:, 0:D], res[:, n, tile, :],
                                            ALU.add).then_inc(summed_ready, 1)
                    dve.wait_ge(summed_ready, w + 1)
                    nc.vector.bn_stats(stats[:, w % 2, :], summed[:, w % 2, :]).then_inc(stats_ready, 1)
                    dve.wait_ge(stats_ready, w + 1)
                    nc.vector.bn_aggr(mv[:, w % 2, :], stats[:, w % 2, :]).then_inc(mv_ready, 1)
                    dve.wait_ge(mv_ready, w + 1)
                    nc.vector.tensor_scalar(veps[:, w % 2:w % 2 + 1], mv[:, w % 2, 1:2], EPS, None,
                                            ALU.add).then_inc(veps_ready, 1)

            def maximum(t):
                if t < UNITS:
                    dve.wait_ge(scores_ready, t + 1)
                    nc.vector.tensor_reduce(top[:, t % 2, :],
                                            scores_ps[:, t % 2].rearrange("p a (h k) -> p (a h) k", k=SEQ),
                                            AX.X, ALU.max).then_inc(max_ready, 1)

            def side_stage(t):
                if side_of(t) is not None:
                    side_read(side_of(t))

            def shift(t):
                if t < UNITS:
                    dve.wait_ge(max_ready, t + 1)
                    if t >= 2:
                        dve.wait_ge(probsT_ready, 2 * (t - 1))
                    nc.vector.tensor_tensor(
                        probs[:, t % 2, :].rearrange("p (h k) -> p h k", k=SEQ),
                        scores_ps[:, t % 2].rearrange("p a (h k) -> p (a h) k", k=SEQ),
                        top[:, t % 2, :].unsqueeze(2).broadcast_to((P, HEADS, SEQ)), ALU.subtract).then_inc(shifted, 1)

            def normalise(t):
                w = t - 3
                if 0 <= w < UNITS:
                    dve.wait_ge(rstd_ready, w + 1)
                    if w >= 2:
                        dve.wait_ge(xnT_ready, w - 1)
                        dve.wait_ge(res_ready, w - 1)
                    nc.vector.tensor_scalar(xn[:, w % 2, :], summed[:, w % 2, :], mv[:, w % 2, 0:1],
                                            rstd[:, w % 2:w % 2 + 1], ALU.subtract, ALU.mult).then_inc(xn_ready, 1)

            def mix(t):
                u = t - 2
                if 0 <= u < UNITS:
                    dve.wait_ge(weighedT_ready, u + 1)
                    wt = dve_ps[:].rearrange("p (h x) -> p h x", x=SEQ)
                    nc.vector.reciprocal(rsum[:, u % 2, :].rearrange("p (h r) -> p h r", r=2),
                                         wt[:, :, 4 * HD:4 * HD + 2]).then_inc(rsum_ready, 1)
                    dve.wait_ge(rsum_ready, u + 1)
                    if u >= 2:
                        dve.wait_ge(mixedT_ready, u - 1)
                    for b in range(2):
                        q = slice(b * SEQ, (b + 1) * SEQ)
                        ins = nc.vector.tensor_tensor(
                            mixed[q, u % 2, :].rearrange("p (h r d) -> p h r d", h=HP, r=2),
                            wt[q, :, b * 2 * HD:(b + 1) * 2 * HD].rearrange("p h (r d) -> p h r d", r=2),
                            rsum[q, u % 2, :].rearrange("p (h r) -> p h r", r=2).unsqueeze(3).broadcast_to((SEQ, HP, 2, HD)),
                            ALU.mult)
                    ins.then_inc(mixed_ready, 1)

            for t in range(LAST):
                maximum(t)
                residual(t)
                side_stage(t)
                shift(t)
                mix(t)
                if t == 1:
                    zero_vals(1)
                normalise(t)

            count = [0]

            def link(ins):
                count[0] += 1
                ins.then_inc(rchain, 1)
                dve.wait_ge(rchain, count[0])

            def over_experts(v):
                return v.unsqueeze(2).broadcast_to((P, TILES, E))

            lg, sh, ex, pr, key, pick1, left, pick2, tmp = (r_buf[:, i] for i in range(9))
            lmax, lsum, m1, dif, e21, den, gate1, gate2 = (r_one[:, i] for i in range(8))
            ranks = rank[:].unsqueeze(1).broadcast_to((P, TILES, E))
            dve.wait_ge(logits_ready, 1)
            dve.wait_ge(small_in, 16 * 4)
            link(nc.vector.tensor_tensor(lg, act_ps[:, LOGITS:LOGITS + TILES * E].rearrange("p (t e) -> p t e", e=E),
                                         rb_bc[:].unsqueeze(1).broadcast_to((P, TILES, E)), ALU.add))
            link(nc.vector.tensor_reduce(lmax, lg, AX.X, ALU.max))
            nc.vector.tensor_tensor(sh, lg, over_experts(lmax), ALU.subtract).then_inc(r_exp_in, 1)
            dve.wait_ge(r_exp, 1)
            link(nc.vector.tensor_reduce(lsum, ex, AX.X, ALU.add))
            link(nc.vector.reciprocal(den, lsum))
            link(nc.vector.tensor_tensor(pr, ex, over_experts(den), ALU.mult))
            link(nc.vector.tensor_reduce(m1, pr, AX.X, ALU.max))

            def pick(src, most, chosen):
                link(nc.vector.tensor_tensor(key, src, over_experts(most), ALU.is_equal))
                link(nc.vector.tensor_tensor(key, key, ranks, ALU.mult))
                link(nc.vector.tensor_reduce(lmax, key, AX.X, ALU.max))
                link(nc.vector.tensor_tensor(chosen, key, over_experts(lmax), ALU.is_equal))

            pick(pr, m1, pick1)
            link(nc.vector.scalar_tensor_tensor(left.rearrange("p t e -> p (t e)"), pick1.rearrange("p t e -> p (t e)"),
                                                -2.0, pr.rearrange("p t e -> p (t e)"), ALU.mult, ALU.add))
            link(nc.vector.tensor_reduce(lsum, left, AX.X, ALU.max))
            nc.vector.tensor_tensor(dif, lsum, m1, ALU.subtract).then_inc(r_exp_in, 1)
            pick(left, lsum, pick2)
            dve.wait_ge(r_exp, 2)
            link(nc.vector.tensor_scalar(den, e21, 1.0, None, ALU.add))
            link(nc.vector.reciprocal(gate1, den))
            link(nc.vector.tensor_tensor(gate2, gate1, e21, ALU.mult))
            link(nc.vector.tensor_tensor(pick1, pick1, over_experts(gate1), ALU.mult))
            link(nc.vector.tensor_tensor(tmp, pick2, over_experts(gate2), ALU.mult))
            nc.vector.tensor_tensor(gate[:], pick1, tmp, ALU.add).then_inc(gate_ready, 1)
            dve.wait_ge(gate_ready, 1)

            def add_expert(g):
                c, e = g // E, g % E
                dve.wait_ge(down_ready, g + 1)
                for j in range(TPC):
                    tile = c * TPC + j
                    if e == 0:
                        nc.vector.tensor_scalar(acc[:, tile, :], probsT_ps[:, g % 2, j * D:(j + 1) * D],
                                                gate[:, tile, e:e + 1], None, ALU.mult).then_inc(acc_ready, 1)
                    else:
                        if j == 0:
                            dve.wait_ge(acc_ready, g * TPC)
                        nc.vector.scalar_tensor_tensor(acc[:, tile, :], probsT_ps[:, g % 2, j * D:(j + 1) * D],
                                                       gate[:, tile, e:e + 1], acc[:, tile, :],
                                                       ALU.mult, ALU.add).then_inc(acc_ready, 1)

            l3 = [0]

            def link3(ins):
                l3[0] += 1
                ins.then_inc(l3chain, 1)

            for g in range(STEPS):
                add_expert(g)
                if g == 1:
                    dve.wait_ge(b2_ready, 1)
                    dve.wait_ge(res_ready, UNITS)
                    for c, bank in enumerate((act_ps, dve_ps)):
                        r = res[:, 2, c * TPC:(c + 1) * TPC, :].rearrange("p t d -> p (t d)")
                        link3(nc.vector.tensor_tensor(r, bank[:, :], r, ALU.add))
                    dve.wait_ge(l3chain, l3[0])
                if g % E == E - 1:
                    c = g // E
                    tiles = range(c * TPC, (c + 1) * TPC)
                    dve.wait_ge(acc_ready, (g + 1) * TPC)
                    s = slice(c * TPC, (c + 1) * TPC)
                    link3(nc.vector.tensor_tensor(acc[:, s, :], acc[:, s, :], res[:, 2, s, :], ALU.add))
                    dve.wait_ge(l3chain, l3[0])
                    for i in tiles:
                        link3(nc.vector.bn_stats(st3[:, i, :], acc[:, i, :]))
                    dve.wait_ge(l3chain, l3[0])
                    for i in tiles:
                        link3(nc.vector.bn_aggr(mv3[:, i, :], st3[:, i, :]))
                    dve.wait_ge(l3chain, l3[0])
                    nc.vector.tensor_scalar(ve3[:, s], mv3[:, s, 1], EPS, None, ALU.add).then_inc(ve3_ready, 1)
                    dve.wait_ge(rstd3_ready, c + 1)
                    for i in tiles:
                        link3(nc.vector.tensor_scalar(acc[:, i, :], acc[:, i, :], mv3[:, i, 0:1], rstd3[:, i:i + 1],
                                                      ALU.subtract, ALU.mult))
                    dve.wait_ge(l3chain, l3[0])
                    link3(nc.vector.tensor_tensor(acc[:, s, :], acc[:, s, :],
                                                  bc["g2"][:].unsqueeze(1).broadcast_to((P, TPC, D)), ALU.mult))
                    dve.wait_ge(l3chain, l3[0])
                    nc.vector.tensor_tensor(y3[:, s, :], acc[:, s, :],
                                            bc["b2"][:].unsqueeze(1).broadcast_to((P, TPC, D)), ALU.add).then_inc(y_ready, 1)

        @block.gpsimd
        def _(pool):
            gc = [0]

            def link(ins):
                gc[0] += 1
                ins.then_inc(chain_g, 1)
                pool.wait_ge(chain_g, gc[0])

            link(nc.gpsimd.memset(own_head[:], 1.0))
            link(nc.gpsimd.affine_select(out=own_head[:], in_=own_head[:], compare_op=ALU.is_ge, fill=0.0, base=0,
                                         pattern=[[-HD, HEADS]], channel_multiplier=1))
            nc.gpsimd.affine_select(out=own_head[:], in_=own_head[:], compare_op=ALU.is_ge, fill=0.0, base=HD - 1,
                                    pattern=[[HD, HEADS]], channel_multiplier=-1).then_inc(consts, 1)
            pool.wait_ge(consts, 1)
            link(nc.gpsimd.memset(ident[:], 0.0))
            nc.gpsimd.affine_select(out=ident[:], in_=ident[:], compare_op=ALU.not_equal, fill=1.0, base=0,
                                    pattern=[[-1, P]], channel_multiplier=1).then_inc(consts, 1)
            pool.wait_ge(consts, 2)
            nc.gpsimd.tensor_copy(ident_bf[:], ident[:]).then_inc(consts, 1)
            pool.wait_ge(consts, 3)
            link(nc.gpsimd.memset(mask_bf[:], 0.0))
            for b in range(2):
                m = mask_bf[b * SEQ:(b + 1) * SEQ, :].rearrange("p (h k) -> p h k", k=SEQ)
                ins = nc.gpsimd.affine_select(out=m, in_=m, compare_op=ALU.is_ge, fill=MASKED, base=0,
                                              pattern=[[0, HP], [-1, SEQ]], channel_multiplier=1)
                if b == 0:
                    link(ins)
            ins.then_inc(consts, 1)
            pool.wait_ge(consts, 4)
            nc.gpsimd.memset(spread[:, 1, :], 0.0).then_inc(zeroed, 1)
            pool.dma_start(b1_rows[:], b1.rearrange("e (k f) -> (e k) f", f=P)).then_inc(b1_in, 16)
            pool.dma_start(bc["g2"][:], ln[2][0].partition_broadcast(P)).then_inc(small_in, 16)
            pool.dma_start(bc["b2"][:], ln[2][1].partition_broadcast(P)).then_inc(small_in, 16)
            pool.dma_start(rb_bc[:], router_b.partition_broadcast(P)).then_inc(small_in, 16)
            pool.dma_start(rw_sb[:], router_w).then_inc(small_in, 16)
            nc.gpsimd.memset(neg_half[:], -0.5).then_inc(consts, 1)
            pool.wait_ge(src_in[0][0], 16)
            pool.wait_ge(src_in[0][1], 16)
            pool.wait_ge(bo0_in, 16)
            nc.gpsimd.tensor_tensor(res[:, 0], x_sb[:], bc["bo0"][:].unsqueeze(1).broadcast_to((P, TILES, D)),
                                    ALU.add).then_inc(res0_ready, 1)
            for e in range(E):
                link(nc.gpsimd.memset(rank[:, e:e + 1], float(E - e)))
            link(nc.gpsimd.memset(b2_bd[:], 0.0))
            for i in range(TILES):
                pool.dma_start(b2_bd[i * E:(i + 1) * E, i * D:(i + 1) * D], b2).then_inc(b2_in, 16)
            pool.wait_ge(lnp_in, 16 * 9)
            link(nc.gpsimd.tensor_tensor(bc["bo1"][:], bc["b0"][:], bc["bo1"][:], ALU.add))
            pool.wait_ge(consts, 5)
            for u in range(UNITS):
                n, tile = u // TILES, u % TILES
                pool.wait_ge(veps_ready, u + 1)
                nc.gpsimd.tensor_tensor(rstd[:, u % 2:u % 2 + 1], veps[:, u % 2:u % 2 + 1], neg_half[:, 0:1],
                                        ALU.pow).then_inc(rstd_ready, 1)
                pool.wait_ge(xn_ready, u + 1)
                nc.gpsimd.tensor_tensor(gx[:], xn[:, u % 2, :], bc[f"g{n}"][:], ALU.mult).then_inc(gx_ready, 1)
                pool.wait_ge(gx_ready, u + 1)
                if u == TILES:
                    pool.wait_ge(*read_count(product("T", 1, 1)))
                nc.gpsimd.tensor_tensor(res[:, n + 1, tile, :], gx[:], (bc["bo1"] if n == 0 else bc["b1"])[:],
                                        ALU.add).then_inc(res_ready, 1)
                if n == 0:
                    pool.wait_ge(w1_hi_ready, tile + 1)
                    nc.gpsimd.tensor_tensor(w1_lo[:, tile, :], w1_raw[:, tile % 2, :], w1_hi[:, tile, :].bitcast(F32),
                                            ALU.subtract).then_inc(w1_lo_ready, 1)
                else:
                    pool.wait_ge(yT_ready, u + 1)
                    c = slice(tile * P, (tile + 1) * P)
                    nc.gpsimd.tensor_copy(y2T_hi[:, c], yT[:, 1, c]).then_inc(y2T_hi_ready, 1)
                    pool.wait_ge(y2T_hi_ready, tile + 1)
                    nc.gpsimd.tensor_tensor(y2T_lo[:, c], yT[:, 1, c], y2T_hi[:, c].bitcast(F32),
                                            ALU.subtract).then_inc(y2T_lo_ready, 1)
            for c in range(CHUNKS):
                s = slice(c * TPC, (c + 1) * TPC)
                pool.wait_ge(ve3_ready, c + 1)
                nc.gpsimd.tensor_tensor(rstd3[:, s], ve3[:, s], neg_half[:, 0:TPC], ALU.pow).then_inc(rstd3_ready, 1)


_NAMES = ["x", "ctx_1024"] + [
    "L0_xattn_" + n for n in (
        "sa_wq sa_bq sa_wk sa_bk sa_wv sa_bv sa_wo sa_bo ca_wq ca_bq ca_wk ca_bk ca_wv ca_bv ca_wo ca_bo "
        "ln1_g ln1_b ln2_g ln2_b ln3_g ln3_b router_w router_b e_w1 e_b1 e_w2 e_b2").split()]


def kernel(**inputs):
    import numpy as np
    import concourse.bacc as bacc
    from concourse.bass_utils import run_bass_kernel_spmd

    nc = bacc.Bacc("TRN2", target_bir_lowering=False, num_devices=1)
    arrays, ap = {}, {}
    for name in _NAMES:
        a = np.ascontiguousarray(inputs[name])
        arrays[f"in_{name}"] = a
        ap[name.replace("L0_xattn_", "")] = nc.dram_tensor(
            f"in_{name}", a.shape, mybir.dt.from_np(a.dtype), kind="ExternalInput").ap()
    shape = inputs["x"].shape
    out = nc.dram_tensor("out_0", shape, F32, kind="ExternalOutput").ap()
    att = [{n: ap[f"{a}_{n}"] for n in ("wq", "bq", "wk", "bk", "wv", "bv", "wo", "bo")} for a in ("sa", "ca")]
    build_decoder_layer(nc, ap["x"], ap["ctx_1024"], att[0], att[1],
                        [(ap[f"ln{i}_g"], ap[f"ln{i}_b"]) for i in (1, 2, 3)],
                        ap["router_w"], ap["router_b"], ap["e_w1"], ap["e_b1"], ap["e_w2"], ap["e_b2"], out)
    r = run_bass_kernel_spmd(nc, [arrays], core_ids=[0])
    return r.results[0]["out_0"]
```

```python
from contextlib import ExitStack

import concourse.bass as bass
from concourse import mybir

F32 = mybir.dt.float32
F32R = mybir.dt.float32r
BF16 = mybir.dt.bfloat16
ALU = mybir.AluOpType
ACT = mybir.ActivationFunctionType
AX = mybir.AxisListType

P = 128
D = 128
SEQ = 64
HEADS = 16
HD = D // HEADS
EPS = 1e-5
MASKED = -1e30


def build_decoder_layer(nc, x, ctx, sa, ca, ln, router_w, router_b, w1, b1, w2, b2, out):
    NSEQ = x.shape[0]
    TILES = NSEQ * SEQ // P
    UNITS = 2 * TILES
    E, _, FF = w1.shape
    FC = FF // P
    CH = 512
    CHUNKS = TILES * P // CH
    TPC = CH // P
    STEPS = CHUNKS * E
    SCALE = float(HD) ** -0.5
    HP = HEADS // 2
    SW = HEADS * SEQ
    SETW = 2 * TPC * SW

    x_tok = x.rearrange("(t b) s d -> (b s) t d", b=2)
    ctx_tok = ctx.rearrange("(t b) s d -> (b s) t d", b=2)
    out_tok = out.rearrange("(t b) s d -> (b s) t d", b=2)
    w1_v = w1.rearrange("e d f -> d e f")
    w2_v = w2.rearrange("e (k p) d -> p e k d", p=P)
    att = [sa, ca]

    with ExitStack() as stack:
        def sb(name, shape, dt=F32):
            return stack.enter_context(nc.sbuf_tensor(name, shape, dt))

        def ps(name, shape):
            return stack.enter_context(nc.psum_tensor(name, shape, F32))

        def sem(name):
            return stack.enter_context(nc.semaphore(name))

        scores_ps = ps("scores_ps", [P, 2, 2, 512])
        probsT_ps = ps("probsT_ps", [P, 2, 512])
        act_ps = ps("act_ps", [P, 512])
        dve_ps = ps("dve_ps", [P, 512])
        LOGITS = 256

        x_sb = sb("x_sb", [P, TILES, D])
        keysT = sb("keysT", [P, 2, NSEQ, SEQ])
        VW = 4 * HD + 2
        vals = sb("vals", [P, 2, TILES, HP, VW])
        wqkvo = {(a, n): sb(f"w{n}{a}", [D, D]) for a in range(2) for n in "qkvo"}
        NB1 = E * FC
        bias_rows = sb("bias_rows", [NB1 + E, D])
        bias_cols = sb("bias_cols", [P, NB1 + E])
        col = {n: sb(f"col_{n}", [D, 1]) for n in ["bq0", "bk0", "bq1", "bk1", "g0", "b0", "g1", "b1"]}
        bc = {n: sb(f"bc_{n}", [P, D]) for n in ["bv0", "bv1", "bo0", "bo1", "g0", "b0", "g2", "b2"]}
        rb_bc = sb("rb_bc", [P, E])
        rw_sb = sb("rw_sb", [D, E])
        select = sb("select", [2 * E, E, P], F32R)
        ident = sb("ident", [P, P])
        ident_bf = sb("ident_bf", [P, P], BF16)
        mask_bf = sb("mask_bf", [P, 512], BF16)
        own_head = sb("own_head", [P, HEADS])
        neg_half = sb("neg_half", [P, TILES])
        rank = sb("rank", [P, E])
        raw_sb = sb("raw_sb", [D, 2, FF])
        w1_hi = sb("w1_hi", [D, E, FF], F32R)
        w1_lo = sb("w1_lo", [D, E, FF], F32R)
        y2T_hi = sb("y2T_hi", [P, TILES * P], F32R)
        y2T_lo = sb("y2T_lo", [P, TILES * P], F32R)

        qT = sb("qT", [P, 2, P])
        top = sb("top", [P, 2, HEADS])
        probs = sb("probs", [P, 2, SW])
        probsT = sb("probsT", [P, 2, SW])
        weighed = sb("weighed", [P, 2, 512])
        rsum = sb("rsum", [P, 2, HEADS])
        mixed = sb("mixed", [P, 2, D])
        mixedT = sb("mixedT", [P, 2, P])
        summed = sb("summed", [P, 2, D])
        stats = sb("stats", [P, 2, 6])
        mv = sb("mv", [P, 2, 2])
        veps = sb("veps", [P, 2])
        rstd = sb("rstd", [P, 2])
        xn = sb("xn", [P, 2, D])
        gx = sb("gx", [P, D])
        res = sb("res", [P, 2, TILES, D])
        ctx_sb = sb("ctx_sb", [P, TILES, D])
        yT = sb("yT", [P, 2, TILES * P])
        r_one = sb("r_one", [P, 8, TILES])
        gate = sb("gate", [P, TILES, E])
        gate_parts = sb("gate_parts", [P, TILES, 2, E], F32R)
        early = ExitStack()

        def early_sb(name, shape):
            return early.enter_context(nc.sbuf_tensor(name, shape, F32))

        spread = early_sb("spread", [P, 2, SETW])
        keys_bd = spread[:].rearrange("p s (b h k) -> p s b h k", h=HEADS, k=SEQ)
        srcT = early_sb("srcT", [P, 2, TILES * P])
        early.close()
        w2_hi, w2_lo = (sb(n, [P, E, FC, D], F32R) for n in ("w2_hi", "w2_lo"))
        h_hi, h_lo = (sb(n, [P, 2 * FC, CH], F32R) for n in ("h_hi", "h_lo"))
        gate_rows = sb("gate_rows", [2 * E, TILES * P], F32R)
        h_raw = probs[:].rearrange("p s (n t) -> p (s n) t", t=CH)
        acc = probsT[:, 0]
        term = probsT[:, 1].rearrange("p (n t) -> p n t", n=2)
        gate_all = yT[:, 0].rearrange("p (n t) -> p n t", n=2)[:, :, 0:CH]
        r_buf = vals[:, 0].rearrange("p t h v -> p (t h v)")[:, 0:9 * TILES * E].rearrange(
            "p (n t e) -> p n t e", n=9, t=TILES)
        normed = weighed[:].rearrange("p c (t d) -> p (c t) d", d=D)
        y3 = x_sb
        RAW = 4

        def raw(i):
            return raw_sb[:, i % 2, :] if i % RAW < 2 else x_sb[:, i % 2 * TPC:(i % 2 + 1) * TPC, :].rearrange("p t d -> p (t d)")
        st3 = sb("st3", [P, TILES, 6])
        mv3 = sb("mv3", [P, TILES, 2])
        ve3 = sb("ve3", [P, TILES])
        rstd3 = sb("rstd3", [P, TILES])

        src_in = [[sem(f"src_in{a}{i}") for i in range(2)] for a in range(2)]
        w_in = {k: sem(f"w_in_{k[1]}{k[0]}") for k in wqkvo}
        col_in = {k: sem(f"col_in_{k}") for k in col if k[0:2] in ("bq", "bk")}
        bv_in = [sem(f"bv_in{a}") for a in range(2)]
        lnp_in, bo0_in, bias_in, small_in, bias_done = (
            sem("lnp_in"), sem("bo0_in"), sem("bias_in"), sem("small_in"), sem("bias_done"))
        biasT_ready = sem("biasT_ready")
        keys0_ready, keys0_used = sem("keys0_ready"), sem("keys0_used")
        keys_in = [sem(f"keys_in{s}") for s in range(4)]
        w1_in = [sem(f"w1_in{e}") for e in range(E)]
        w2_in = [sem(f"w2_in{e}") for e in range(E)]
        zeroed, vals_zeroed = sem("zeroed"), [sem(f"vals_zeroed{a}") for a in range(2)]
        consts = sem("consts")
        pro_ready, pro_act, pro_dve = sem("pro_ready"), sem("pro_act"), sem("pro_dve")
        spread_act, spread_dve = sem("spread_act"), sem("spread_dve")
        q_ready, q_used = sem("q_ready"), sem("q_used")
        scores_ready, max_ready, shifted = sem("scores_ready"), sem("max_ready"), sem("shifted")
        probs_ready, probsT_ready, probsT_copied = sem("probs_ready"), sem("probsT_ready"), sem("probsT_copied")
        pv_ready, weighed_ready, weighedT_ready = sem("pv_ready"), sem("weighed_ready"), sem("weighedT_ready")
        rsum_ready, mixed_ready = sem("rsum_ready"), sem("mixed_ready")
        mixedT_ready, mixedT_used = sem("mixedT_ready"), sem("mixedT_used")
        proj_ready, summed_ready, stats_ready = sem("proj_ready"), sem("summed_ready"), sem("stats_ready")
        mv_ready, veps_ready, rstd_ready = sem("mv_ready"), sem("veps_ready"), sem("rstd_ready")
        xn_ready, xnT_ready, yT_ready = sem("xn_ready"), sem("xnT_ready"), sem("yT_ready")
        res0_ready, gx_ready, res_ready = sem("res0_ready"), sem("gx_ready"), sem("res_ready")
        w1_hi_ready, w1_lo_ready = sem("w1_hi_ready"), sem("w1_lo_ready")
        y2T_hi_ready, y2T_lo_ready = sem("y2T_hi_ready"), sem("y2T_lo_ready")
        logits_ready, logits_used, rchain, r_exp_in, r_exp = sem("logits_ready"), sem("logits_used"), sem("rchain"), sem("r_exp_in"), sem("r_exp")
        gate_parts_ready = sem("gate_parts_ready")
        gateT_ready, gate_rows_ready, gate_all_ready = sem("gateT_ready"), sem("gate_rows_ready"), sem("gate_all_ready")
        w2_hi_ready, w2_lo_ready, h_hi_ready, h_lo_ready = (
            sem("w2_hi_ready"), sem("w2_lo_ready"), sem("h_hi_ready"), sem("h_lo_ready"))
        gate_cast, select_ready, term_ready, accT_ready, accT_used = sem("gate_cast"), sem("select_ready"), sem("term_ready"), sem("accT_ready"), sem("accT_used")
        up_ready, gelu_ready, down_ready, acc_ready = sem("up_ready"), sem("gelu_ready"), sem("down_ready"), sem("acc_ready")
        l3chain, ve3_ready, rstd3_ready, y_ready, stored = (
            sem("l3chain"), sem("ve3_ready"), sem("rstd3_ready"), [sem(f"y_ready{p}") for p in range(CHUNKS + 1)], sem("stored"))
        chain_g = sem("chain_g")

        side = [("T", 0, 0, "dve", None), ("T", 0, 1, "act", None), ("K", 0, 0, "act", None),
                ("K", 0, 1, "act", None), ("V", 0, 0, "dve", None), ("V", 0, 1, "dve", None),
                ("V", 0, 2, "dve", 1), ("V", 0, 3, "dve", 2), ("T", 1, 0, "act", 3), ("K", 1, 0, "act", 4),
                ("T", 1, 1, "act", 5), ("K", 1, 1, "act", 6)] + [("V", 1, g, "dve", 7 + g) for g in range(4)]
        OPENING = [n for n, o in enumerate(side) if o[4] is None]

        def side_bank(n):
            if side[n][4] is not None:
                return scores_ps[:, (side[n][4] + 1) % 2, 0, :]
            return scores_ps[:, n // 2, n % 2, :] if n < 4 else probsT_ps[:, n - 4, :]

        def read_count(n):
            who = side[n][3]
            return (pro_act if who == "act" else pro_dve), sum(o[3] == who for o in side[:n + 1])

        def product(what, a, part):
            return next(n for n, o in enumerate(side) if o[:3] == (what, a, part))

        def side_of(rnd):
            return next((n for n, o in enumerate(side) if o[4] == rnd), None)

        B1_ROUND = TILES + 4
        ACT_HEADS = 6
        FIRST_SPREAD = [slice(0, 2), slice(2, 4), slice(4, 2 * TPC)]

        PARTS = [(c * TPC, TPC) for c in range(CHUNKS - 1)] + [(TILES - TPC, TPC // 2), (TILES - TPC // 2, TPC // 2)]
        LATE = len(PARTS) - 1

        def summed_bank(p):
            return probsT_ps[:, (E - 1) % 2, :] if p < LATE - 1 else scores_ps[:, 0, p - LATE + 1, :]

        cast_bank = [dve_ps, act_ps]

        def up_bank(n):
            return scores_ps[:, n % 2, n % FC // 2, :]

        EXP1_STEP, EXP2_STEP, ROWS_STEP = 2, 3, E - 2

        block = stack.enter_context(nc.Block())

        @block.sync
        def _(sp):
            half = TILES // 2

            def column(n, v):
                return sp.dma_start(col[n][:], v.rearrange("(d a) -> d a", a=1))

            def load_w(a, n):
                sp.dma_start(wqkvo[a, n][:], att[a]["w" + n]).then_inc(w_in[a, n], 16)

            def load_src(a, i):
                dst, src = ((x_sb, x_tok), (ctx_sb, ctx_tok))[a]
                sp.dma_start(dst[:, i * half:(i + 1) * half, :], src[:, i * half:(i + 1) * half, :]).then_inc(src_in[a][i], 16)

            load_src(0, 0)
            load_w(0, "k")
            load_src(0, 1)
            column("bk0", sa["bk"]).then_inc(col_in["bk0"], 16)
            load_w(0, "q")
            column("bq0", sa["bq"]).then_inc(col_in["bq0"], 16)
            load_w(0, "v")
            sp.dma_start(bc["bv0"][:], sa["bv"].partition_broadcast(P)).then_inc(bv_in[0], 16)
            load_w(0, "o")
            sp.dma_start(bc["bo0"][:], sa["bo"].partition_broadcast(P)).then_inc(bo0_in, 16)

            def load_expert(i):
                if i in (2, 3):
                    sp.wait_ge(res0_ready, 1)
                elif i >= RAW + E:
                    sp.wait_ge(w2_lo_ready, i - RAW - E + 1)
                elif i >= RAW:
                    sp.wait_ge(w1_lo_ready, i - RAW + 1)
                if i < E:
                    sp.dma_start(raw(i), w1_v[:, i, :]).then_inc(w1_in[i], 16)
                else:
                    sp.dma_start(raw(i).rearrange("p (k d) -> p k d", d=D), w2_v[:, i - E, :, :]).then_inc(w2_in[i - E], 16)

            def spread_keys(s):
                a, part = s // 2, s % 2
                sem_, v = read_count(product("K", a, part))
                sp.wait_ge(sem_, v)
                sp.wait_ge(zeroed, 1)
                if s >= 2:
                    sp.wait_ge(scores_ready, (s - 1) * TPC)
                for h in range(HEADS):
                    r = slice(h * HD, (h + 1) * HD)
                    sp.dma_start(keys_bd[r, s % 2, :, h, :], keysT[r, a, part * 8:part * 8 + 8, :]).then_inc(keys_in[s], 16)

            for n in range(2):
                column(f"g{n}", ln[n][0]).then_inc(lnp_in, 16)
                column(f"b{n}", ln[n][1]).then_inc(lnp_in, 16)
                if n == 0:
                    sp.dma_start(bc["g0"][:], ln[0][0].partition_broadcast(P)).then_inc(lnp_in, 16)
                    sp.dma_start(bc["b0"][:], ln[0][1].partition_broadcast(P)).then_inc(lnp_in, 16)
            sp.dma_start(bc["bo1"][:], ca["bo"].partition_broadcast(P)).then_inc(lnp_in, 16)
            load_src(1, 0)
            load_src(1, 1)
            load_w(1, "k")
            column("bk1", ca["bk"]).then_inc(col_in["bk1"], 16)
            load_expert(0)
            load_expert(1)
            load_w(1, "v")
            sp.dma_start(bc["bv1"][:], ca["bv"].partition_broadcast(P)).then_inc(bv_in[1], 16)
            load_w(1, "q")
            column("bq1", ca["bq"]).then_inc(col_in["bq1"], 16)
            load_w(1, "o")
            spread_keys(1)
            load_expert(2)
            load_expert(3)
            load_expert(4)
            spread_keys(2)
            load_expert(5)
            load_expert(6)
            load_expert(7)
            spread_keys(3)
            for e in range(E):
                load_expert(E + e)
            for p, (i, n) in enumerate(PARTS):
                sp.wait_ge(y_ready[p], 1)
                sp.dma_start(out_tok[:, i:i + n, :], y3[:, i:i + n, :]).then_inc(stored, 16)
            sp.wait_ge(stored, 16 * len(PARTS))

        @block.scalar
        def _(act):
            def side_read(n):
                what, a, part, who, _ = side[n]
                if who != "act":
                    return
                act.wait_ge(pro_ready, n + 1)
                if what == "T":
                    nc.scalar.copy(srcT[:, a, part * 512:part * 512 + 512], side_bank(n)).then_inc(pro_act, 1)
                else:
                    act.wait_ge(col_in[f"bk{a}"], 16)
                    skip = 2 if (a, part) == (0, 0) else 0
                    nc.scalar.activation(
                        keysT[:, a, part * 8 + skip:part * 8 + 8, :],
                        side_bank(n).rearrange("p (b k) -> p b k", k=SEQ)[:, skip:, :],
                        ACT.Identity, bias=col[f"bk{a}"][:]).then_inc(pro_act, 1)

            def q_copy(u):
                a = u // TILES
                act.wait_ge(q_ready, u + 1)
                act.wait_ge(col_in[f"bq{a}"], 16)
                if u >= 2:
                    act.wait_ge(scores_ready, u - 1)
                nc.scalar.activation(qT[:, u % 2, :], act_ps[:, 0:P], ACT.Identity,
                                     bias=col[f"bq{a}"][:]).then_inc(q_used, 1)

            def spread_first(b):
                for h in range(ACT_HEADS):
                    nc.scalar.activation(keys_bd[:, 0, b, h, :], keysT[:, 0, b, :], ACT.Copy,
                                         scale=own_head[:, h:h + 1]).then_inc(spread_act, 1)

            side_read(1)
            act.wait_ge(keys0_ready, 1)
            act.wait_ge(col_in["bk0"], 16)
            nc.scalar.activation(keysT[:, 0, 0:2, :], dve_ps[:, 0:P].rearrange("p (b k) -> p b k", k=SEQ),
                                 ACT.Identity, bias=col["bk0"][:]).then_inc(keys0_used, 1)
            q_copy(0)
            act.wait_ge(keys0_used, 1)
            act.wait_ge(consts, 1)
            spread_first(FIRST_SPREAD[0])
            side_read(2)
            act.wait_ge(pro_act, 2)
            spread_first(FIRST_SPREAD[1])
            side_read(3)
            spread_first(FIRST_SPREAD[2])

            def mixedT_copy(t):
                u = t - 3
                if 0 <= u < UNITS:
                    act.wait_ge(mixedT_ready, u + 1)
                    if u >= 2:
                        act.wait_ge(proj_ready, u - 1)
                    nc.scalar.copy(mixedT[:, u % 2, :], act_ps[:, 0:P]).then_inc(mixedT_used, 1)

            def yT_copy(t):
                u = t - 4
                if u >= 0:
                    n, tile = u // TILES, u % TILES
                    act.wait_ge(xnT_ready, u + 1)
                    if u == 0:
                        act.wait_ge(lnp_in, 16 * 7)
                    nc.scalar.activation(yT[:, n, tile * P:(tile + 1) * P], act_ps[:, 0:P], ACT.Identity,
                                         bias=col[f"b{n}"][:], scale=col[f"g{n}"][:]).then_inc(yT_ready, 1)

            def weighed_copy(t):
                u = t - 2
                if 0 <= u < UNITS:
                    act.wait_ge(pv_ready, u + 1)
                    if u >= 2:
                        act.wait_ge(weighedT_ready, u - 1)
                    nc.scalar.copy(weighed[:, u % 2, :], scores_ps[:, (t + 1) % 2, 1, :]).then_inc(weighed_ready, 1)

            def queries(t):
                if t + 1 < UNITS:
                    q_copy(t + 1)
                if t == B1_ROUND:
                    act.wait_ge(biasT_ready, 1)
                    nc.scalar.copy(bias_cols[:], act_ps[:, 128:128 + NB1 + E]).then_inc(bias_done, 1)

            def probsT_copy(t):
                u = t - 1
                if 0 <= u < UNITS:
                    if u >= 2:
                        act.wait_ge(pv_ready, u - 1)
                    for half in range(2):
                        act.wait_ge(probsT_ready, 2 * u + half + 1)
                        nc.scalar.copy(probsT[:, u % 2, half * 512:half * 512 + 512],
                                       probsT_ps[:, half, :]).then_inc(probsT_copied, 1)

            def side_stage(t):
                if side_of(t) is not None:
                    side_read(side_of(t))

            def exponentials(t):
                if t < UNITS:
                    act.wait_ge(shifted, t + 1)
                    nc.scalar.activation(probs[:, t % 2, :], probs[:, t % 2, :], ACT.Exp,
                                         scale=SCALE).then_inc(probs_ready, 1)

            def w1_leading(t):
                e = t - 2
                if 0 <= e < E:
                    act.wait_ge(w1_in[e], 16)
                    nc.scalar.copy(w1_hi[:, e, :], raw(e)).then_inc(w1_hi_ready, 1)
                if 3 * TPC <= t < UNITS:
                    w2_leading(t - 3 * TPC)

            def w2_leading(e):
                act.wait_ge(w2_in[e], 16)
                act.wait_ge(scores_ready, 3 * TPC)
                nc.scalar.copy(w2_hi[:, e].rearrange("p k d -> p (k d)"), raw(E + e)).then_inc(w2_hi_ready, 1)

            for t in range(UNITS):
                mixedT_copy(t)
                yT_copy(t)
                side_stage(t)
                weighed_copy(t)
                queries(t)
                probsT_copy(t)
                exponentials(t)
                w1_leading(t)

            def router_exp(c, i):
                tiles = slice(c * TPC, (c + 1) * TPC)
                act.wait_ge(r_exp_in, 2 * c + i + 1)
                if i == 0:
                    nc.scalar.activation(r_buf[:, 2, tiles], r_buf[:, 1, tiles], ACT.Exp).then_inc(r_exp, 1)
                else:
                    nc.scalar.activation(r_one[:, 4, tiles], r_one[:, 3, tiles], ACT.Tanh, scale=-0.5).then_inc(r_exp, 1)

            def leading(n):
                act.wait_ge(gelu_ready, n + 1)
                if n >= 2 * FC:
                    act.wait_ge(down_ready, n // FC - 1)
                nc.scalar.copy(h_hi[:, n % (2 * FC), :], h_raw[:, n % 4, :]).then_inc(h_hi_ready, 1)

            def gelu(n):
                act.wait_ge(up_ready, n + 1)
                if n >= 4:
                    act.wait_ge(h_lo_ready, n - 3)
                i = n % NB1
                nc.scalar.activation(h_raw[:, n % 4, :], up_bank(n), ACT.Gelu,
                                     bias=bias_cols[:, i:i + 1]).then_inc(gelu_ready, 1)
                if n % FC > 0:
                    leading(n - 1)

            def gate_copy(g):
                act.wait_ge(gate_cast, g + 1)
                if g >= 2:
                    act.wait_ge(term_ready, g - 1)
                nc.scalar.copy(gate_all[:, g % 2, :], cast_bank[g % 2][:, :]).then_inc(gate_all_ready, 1)

            def rows_copy(c):
                act.wait_ge(gateT_ready, c + 1)
                nc.scalar.copy(gate_rows[:, c * CH:(c + 1) * CH], cast_bank[0][0:2 * E, :]).then_inc(gate_rows_ready, 1)

            mixedT_copy(UNITS)
            router_exp(0, 0)
            weighed_copy(UNITS)
            probsT_copy(UNITS)
            yT_copy(UNITS)
            weighed_copy(UNITS + 1)
            mixedT_copy(UNITS + 1)
            router_exp(0, 1)
            gelu(0)
            gelu(1)
            yT_copy(UNITS + 1)
            mixedT_copy(UNITS + 2)
            gelu(2)
            gelu(3)
            leading(3)
            gelu(4)
            yT_copy(UNITS + 2)
            rows_copy(0)
            gelu(5)
            gelu(6)
            gelu(7)
            yT_copy(UNITS + 3)
            leading(7)
            gate_copy(0)

            for g in range(2, STEPS):
                for n in range(g * FC, (g + 1) * FC):
                    gelu(n)
                gate_copy(g - 1)
                leading((g + 1) * FC - 1)
                if g + 2 < E:
                    w2_leading(g + 2)
                if g in (EXP1_STEP, EXP2_STEP):
                    router_exp(1, int(g == EXP2_STEP))
                if g == ROWS_STEP:
                    rows_copy(1)
            gate_copy(STEPS - 1)

        @block.tensor
        def _(pe):
            src_sb = [x_sb, ctx_sb]

            def side_product(n):
                what, a, part, who, rnd = side[n]
                bank = side_bank(n)
                if what == "T":
                    pe.wait_ge(src_in[a][part], 16)
                    for j in range(4):
                        mm = nc.tensor.transpose(bank[:, j * P:(j + 1) * P], src_sb[a][:, part * 4 + j, :], ident[:])
                elif what == "K":
                    s, v = read_count(product("T", a, part))
                    pe.wait_ge(s, v)
                    pe.wait_ge(w_in[a, "k"], 16)
                    skip = P if (a, part) == (0, 0) else 0
                    mm = nc.tensor.matmul(bank[:, skip:], wqkvo[a, "k"][:],
                                          srcT[:, a, part * 512 + skip:part * 512 + 512], start=True, stop=True)
                else:
                    s, v = read_count(product("T", a, part // 2))
                    pe.wait_ge(s, v)
                    pe.wait_ge(w_in[a, "v"], 16)
                    for j in range(4):
                        b = part * 4 + j
                        for r in range(2):
                            mm = nc.tensor.matmul(bank[r * SEQ:(r + 1) * SEQ, j * D:(j + 1) * D],
                                                  srcT[:, a, b * SEQ:(b + 1) * SEQ], wqkvo[a, "v"][:],
                                                  start=True, stop=True)
                mm.then_inc(pro_ready, 1)

            def q_product(u):
                a, tile = u // TILES, u % TILES
                pe.wait_ge(w_in[a, "q"], 16)
                if a == 0:
                    rhs = srcT[:, 0, tile * P:(tile + 1) * P]
                    if tile % TPC == 0:
                        s, v = read_count(product("T", 0, tile // TPC))
                        pe.wait_ge(s, v)
                else:
                    pe.wait_ge(yT_ready, tile + 1)
                    rhs = yT[:, 0, tile * P:(tile + 1) * P]
                nc.tensor.matmul(act_ps[:, 0:P], wqkvo[a, "q"][:], rhs, start=True, stop=True).then_inc(q_ready, 1)

            pe.wait_ge(consts, 2)
            for n in OPENING[:2]:
                side_product(n)
            pe.wait_ge(*read_count(0))
            pe.wait_ge(w_in[0, "k"], 16)
            nc.tensor.matmul(dve_ps[:, 0:P], wqkvo[0, "k"][:], srcT[:, 0, 0:P], start=True, stop=True).then_inc(keys0_ready, 1)
            q_product(0)
            for n in OPENING[2:4]:
                side_product(n)
            pe.wait_ge(consts, 4)

            def scores(t, half):
                if t >= UNITS:
                    return
                slot = t % 2
                a, s = t // TILES, t // TPC
                if half == 0:
                    pe.wait_ge(q_used, t + 1)
                    if s == 0:
                        pe.wait_ge(spread_act, ACT_HEADS * min(t + 1, len(FIRST_SPREAD)))
                        pe.wait_ge(spread_dve, (HEADS - ACT_HEADS) * min(t + 1, len(FIRST_SPREAD)))
                    else:
                        pe.wait_ge(keys_in[s], 16 * HEADS)
                    if t < 2:
                        for n in OPENING[2 * t:2 * t + 2]:
                            pe.wait_ge(*read_count(n))
                    else:
                        pe.wait_ge(shifted, t - 1)
                        if t >= 3:
                            pe.wait_ge(weighed_ready, t - 2)
                    if side_of(t - 1) is not None:
                        pe.wait_ge(*read_count(side_of(t - 1)))
                o = scores_ps[:, slot, half, :]
                if a == 0:
                    nc.tensor.matmul(o, ident_bf[:], mask_bf[:], start=True, stop=False, skip_group_check=True)
                for b in range(2):
                    mm = nc.tensor.matmul(
                        o[b * SEQ:(b + 1) * SEQ, :], qT[:, slot, b * SEQ:(b + 1) * SEQ],
                        keys_bd[:, s % 2, 2 * (t % TPC) + b, half * HP:(half + 1) * HP, :],
                        start=(a == 1), stop=True, skip_group_check=True)
                if half == 1:
                    mm.then_inc(scores_ready, 1)

            def mixed_transpose(t):
                u, w = t - 4, t - 3
                if 0 <= w < UNITS:
                    pe.wait_ge(mixed_ready, w + 1)
                    if u - 1 >= 0:
                        pe.wait_ge(yT_ready, u)
                    if t == UNITS:
                        pe.wait_ge(logits_used, 1)
                    nc.tensor.transpose(act_ps[:, 0:P], mixed[:, w % 2, :], ident[:]).then_inc(mixedT_ready, 1)

            def project(t):
                w = t - 3
                if 0 <= w < UNITS:
                    pe.wait_ge(mixedT_used, w + 1)
                    pe.wait_ge(w_in[w // TILES, "o"], 16)
                    nc.tensor.matmul(dve_ps[:, 0:D], mixedT[:, w % 2, :], wqkvo[w // TILES, "o"][:],
                                     start=True, stop=True).then_inc(proj_ready, 1)

            def xn_transpose(t):
                u = t - 4
                if u >= 0:
                    pe.wait_ge(xn_ready, u + 1)
                    nc.tensor.transpose(act_ps[:, 0:P], xn[:, u % 2, :], ident[:]).then_inc(xnT_ready, 1)

            def side_stage(t):
                if side_of(t) is not None:
                    if t >= 1:
                        pe.wait_ge(shifted, t)
                    else:
                        for n in OPENING[2:4]:
                            pe.wait_ge(*read_count(n))
                    side_product(side_of(t))

            def weigh(t):
                v, other = t - 2, (t + 1) % 2
                if 0 <= v < UNITS:
                    a, tile = v // TILES, v % TILES
                    pe.wait_ge(probsT_copied, 2 * v + 2)
                    pe.wait_ge(pro_dve, read_count(product("V", a, tile // 2))[1])
                    pe.wait_ge(shifted, min(t, UNITS))
                    for hp in range(HP):
                        r = (hp % 2) * SEQ
                        mm = nc.tensor.matmul(
                            scores_ps[r:r + VW, other, 1, (hp // 2) * P:(hp // 2 + 1) * P],
                            vals[:, a, tile, hp, :], probsT[:, v % 2, hp * P:(hp + 1) * P], start=True, stop=True)
                    mm.then_inc(pv_ready, 1)

            def queries(t):
                u, w = t - 4, t - 3
                if t + 1 < UNITS:
                    if u >= 0:
                        pe.wait_ge(yT_ready, u + 1)
                    elif w >= 0:
                        pe.wait_ge(mixedT_used, w + 1)
                    if t == B1_ROUND:
                        pe.wait_ge(bias_in, 16 * 2)
                        nc.tensor.transpose(act_ps[:, 128:128 + NB1 + E], bias_rows[:],
                                            ident[0:NB1 + E, 0:NB1 + E]).then_inc(biasT_ready, 1)
                    q_product(t + 1)

            def probs_transpose(t):
                p = t - 1
                if 0 <= p < UNITS:
                    pe.wait_ge(probs_ready, p + 1)
                    for half in range(2):
                        if p >= 1:
                            pe.wait_ge(probsT_copied, 2 * p - 1 + half)
                        else:
                            pe.wait_ge(*read_count(OPENING[4 + half]))
                        for j in range(4):
                            hp = half * 4 + j
                            mm = nc.tensor.transpose(probsT_ps[:, half, j * P:(j + 1) * P],
                                                     probs[:, p % 2, hp * P:(hp + 1) * P], ident[:])
                        mm.then_inc(probsT_ready, 1)

            def logits(t):
                u = t - 4
                if u >= TILES:
                    tile = u % TILES
                    if u == TILES:
                        pe.wait_ge(small_in, 16 * 4)
                        pe.wait_ge(bias_done, 1)
                    pe.wait_ge(yT_ready, u + 1 if t < UNITS else UNITS)
                    if t + 1 < UNITS:
                        pe.wait_ge(q_used, t + 2)
                    mm = nc.tensor.matmul(act_ps[:, LOGITS + tile * E:LOGITS + (tile + 1) * E],
                                          yT[:, 1, tile * P:(tile + 1) * P], rw_sb[:], start=True, stop=True)
                    if tile % TPC == TPC - 1:
                        mm.then_inc(logits_ready, 1)

            def weighed_transpose(t):
                v, w = t - 2, t - 3
                if 0 <= v < UNITS:
                    pe.wait_ge(weighed_ready, v + 1)
                    if w >= 0:
                        pe.wait_ge(summed_ready, w + 1)
                    for r in range(4):
                        mm = nc.tensor.transpose(dve_ps[:, r * P:(r + 1) * P], weighed[:, v % 2, r * P:(r + 1) * P], ident[:])
                    mm.then_inc(weighedT_ready, 1)

            for t in range(UNITS):
                scores(t, 0)
                mixed_transpose(t)
                scores(t, 1)
                if t == 0:
                    side_product(4)
                    side_product(5)
                project(t)
                side_stage(t)
                xn_transpose(t)
                weigh(t)
                queries(t)
                probs_transpose(t)
                weighed_transpose(t)
                logits(t)

            def up(n):
                c, e, k = n // FC // E, n // FC % E, n % FC
                pe.wait_ge(w1_lo_ready, e + 1)
                pe.wait_ge(y2T_lo_ready, (c + 1) * TPC)
                if n < 2:
                    pe.wait_ge(shifted, UNITS - 1 + n)
                elif n < 4:
                    pe.wait_ge(weighed_ready, UNITS + 2 - n)
                else:
                    pe.wait_ge(gelu_ready, n - FC + 1)
                f = slice(k * P, (k + 1) * P)
                tok = slice(c * CH, (c + 1) * CH)
                nc.tensor.matmul(up_bank(n), w1_hi[:, e, f], y2T_hi[:, tok], start=True, stop=False)
                nc.tensor.matmul(up_bank(n), w1_hi[:, e, f], y2T_lo[:, tok], start=False, stop=False)
                nc.tensor.matmul(up_bank(n), w1_lo[:, e, f], y2T_hi[:, tok], start=False, stop=True).then_inc(up_ready, 1)

            def down(g):
                e = g % E
                pe.wait_ge(w2_lo_ready, e + 1)
                if g >= 2:
                    pe.wait_ge(term_ready, g - 1)
                if g == E + 1:
                    pe.wait_ge(accT_used, 1)
                halves = 2 if g == STEPS - 1 else 1
                for half in range(halves):
                    t = slice(half * CH // 2, (half + 1) * CH // 2) if halves == 2 else slice(0, CH)
                    if half == 1:
                        pe.wait_ge(term_ready, g)
                    for k in range(FC):
                        n = g * FC + k
                        pe.wait_ge(h_lo_ready, n + 1)
                        for i, (w, h) in enumerate(((w2_hi, h_hi), (w2_lo, h_hi), (w2_hi, h_lo))):
                            mm = nc.tensor.matmul(probsT_ps[:, (g + half) % 2, t], w[:, e, k, :], h[:, n % (2 * FC), t],
                                                  start=(k == 0 and i == 0), stop=(k == FC - 1 and i == 2))
                    mm.then_inc(down_ready, 1)

            def cast_gate(g):
                c, e = g // E, g % E
                if g == 0:
                    pe.wait_ge(select_ready, 1)
                if g == 1:
                    pe.wait_ge(yT_ready, UNITS)
                    pe.wait_ge(logits_used, CHUNKS)
                if g >= 2:
                    pe.wait_ge(gate_all_ready, g - 1)
                pe.wait_ge(gate_rows_ready, 1 if g < ROWS_STEP else CHUNKS)
                nc.tensor.matmul(cast_bank[g % 2][:, :], select[:, e, :], gate_rows[:, c * CH:(c + 1) * CH],
                                 start=True, stop=True).then_inc(gate_cast, 1)

            def transpose_sum(p):
                i, n = PARTS[p]
                pe.wait_ge(acc_ready, {LATE: STEPS + 1, LATE - 1: STEPS}.get(p, (p + 1) * E))
                for j in range(n):
                    mm = nc.tensor.transpose(summed_bank(p)[:, j * P:(j + 1) * P],
                                             acc[:, (i + j) * P:(i + j + 1) * P], ident[:])
                mm.then_inc(accT_ready, 1)

            def gate_transpose(c):
                pe.wait_ge(gate_parts_ready, 2 * (c + 1))
                if c == 0:
                    pe.wait_ge(summed_ready, UNITS)
                else:
                    pe.wait_ge(gate_all_ready, ROWS_STEP - 1)
                for j in range(TPC):
                    mm = nc.tensor.transpose(cast_bank[0][0:2 * E, j * P:(j + 1) * P],
                                             gate_parts[:, c * TPC + j].bitcast(F32).rearrange("p n e -> p (n e)"), ident[:])
                mm.then_inc(gateT_ready, 1)

            weigh(UNITS)
            up(0)
            probs_transpose(UNITS)
            mixed_transpose(UNITS)
            project(UNITS)
            weighed_transpose(UNITS)
            weigh(UNITS + 1)
            xn_transpose(UNITS)
            up(1)
            mixed_transpose(UNITS + 1)
            up(2)
            project(UNITS + 1)
            up(3)
            xn_transpose(UNITS + 1)
            weighed_transpose(UNITS + 1)
            up(4)
            mixed_transpose(UNITS + 2)
            project(UNITS + 2)
            xn_transpose(UNITS + 2)
            up(5)
            gate_transpose(0)
            up(6)
            up(7)
            cast_gate(0)
            xn_transpose(UNITS + 3)
            down(0)
            logits(UNITS)
            logits(UNITS + 1)
            logits(UNITS + 2)
            logits(UNITS + 3)

            for g in range(2, STEPS + 1):
                if g < STEPS:
                    for n in range(g * FC, (g + 1) * FC):
                        up(n)
                cast_gate(g - 1)
                down(g - 1)
                if g == ROWS_STEP:
                    gate_transpose(1)
                if g == E + 1:
                    transpose_sum(0)
            transpose_sum(1)
            transpose_sum(2)

        @block.vector
        def _(dve):
            def side_read(n):
                what, a, part, who, _ = side[n]
                if who != "dve":
                    return
                dve.wait_ge(pro_ready, n + 1)
                if what == "T":
                    nc.vector.tensor_copy(srcT[:, a, part * 512:part * 512 + 512], side_bank(n)).then_inc(pro_dve, 1)
                    return
                dve.wait_ge(bv_in[a], 16)
                dve.wait_ge(vals_zeroed[a], 3)
                for par in range(2):
                    r = slice(par * SEQ, (par + 1) * SEQ)
                    for b in range(2):
                        src = side_bank(n)[r, :].rearrange("p (t b h r d) -> p t b h r d", t=2, b=2, h=HP, r=2)[:, :, b, :, par, :]
                        bias = bc[f"bv{a}"][r, :].rearrange("p (h r d) -> p h r d", h=HP, r=2)[:, :, par, :]
                        bias = bias.unsqueeze(1).broadcast_to((SEQ, 2, HP, HD))
                        c = (b * 2 + par) * HD
                        ins = nc.vector.tensor_tensor(vals[r, a, part * 2:part * 2 + 2, :, c:c + HD], src, bias, ALU.add)
                ins.then_inc(pro_dve, 1)

            nc.vector.memset(vals[:, 0].rearrange("p t h v -> p (t h v)"), 0.0).then_inc(vals_zeroed[0], 1)
            dve.wait_ge(vals_zeroed[0], 1)
            for par in range(2):
                nc.vector.memset(vals[par * SEQ:(par + 1) * SEQ, 0, :, :, 4 * HD + par], 1.0).then_inc(vals_zeroed[0], 1)
            side_read(0)
            dve.wait_ge(consts, 1)

            def spread_first(b):
                for h in range(ACT_HEADS, HEADS):
                    nc.vector.tensor_scalar(keys_bd[:, 0, b, h, :], keysT[:, 0, b, :], own_head[:, h:h + 1], None,
                                            ALU.mult).then_inc(spread_dve, 1)

            dve.wait_ge(keys0_used, 1)
            spread_first(FIRST_SPREAD[0])
            dve.wait_ge(pro_act, 2)
            spread_first(FIRST_SPREAD[1])

            def residual(t):
                w = t - 3
                if 0 <= w < UNITS:
                    n, tile = w // TILES, w % TILES
                    dve.wait_ge(proj_ready, w + 1)
                    if w == 0:
                        dve.wait_ge(res0_ready, 1)
                    if n == 1:
                        dve.wait_ge(res_ready, tile + 1)
                    nc.vector.tensor_tensor(summed[:, w % 2, :], dve_ps[:, 0:D], res[:, n, tile, :],
                                            ALU.add).then_inc(summed_ready, 1)
                    dve.wait_ge(summed_ready, w + 1)
                    nc.vector.bn_stats(stats[:, w % 2, :], summed[:, w % 2, :]).then_inc(stats_ready, 1)
                    dve.wait_ge(stats_ready, w + 1)
                    nc.vector.bn_aggr(mv[:, w % 2, :], stats[:, w % 2, :]).then_inc(mv_ready, 1)
                    dve.wait_ge(mv_ready, w + 1)
                    nc.vector.tensor_scalar(veps[:, w % 2:w % 2 + 1], mv[:, w % 2, 1:2], EPS, None,
                                            ALU.add).then_inc(veps_ready, 1)

            def maximum(t):
                if t < UNITS:
                    dve.wait_ge(scores_ready, t + 1)
                    nc.vector.tensor_reduce(top[:, t % 2, :],
                                            scores_ps[:, t % 2].rearrange("p a (h k) -> p (a h) k", k=SEQ),
                                            AX.X, ALU.max).then_inc(max_ready, 1)

            def side_stage(t):
                if side_of(t) is not None:
                    side_read(side_of(t))

            def shift(t):
                if t < UNITS:
                    dve.wait_ge(max_ready, t + 1)
                    if t >= 2:
                        dve.wait_ge(probsT_ready, 2 * (t - 1))
                    nc.vector.tensor_tensor(
                        probs[:, t % 2, :].rearrange("p (h k) -> p h k", k=SEQ),
                        scores_ps[:, t % 2].rearrange("p a (h k) -> p (a h) k", k=SEQ),
                        top[:, t % 2, :].unsqueeze(2).broadcast_to((P, HEADS, SEQ)), ALU.subtract).then_inc(shifted, 1)

            def normalise(t):
                w = t - 3
                if 0 <= w < UNITS:
                    dve.wait_ge(rstd_ready, w + 1)
                    if w >= 2:
                        dve.wait_ge(xnT_ready, w - 1)
                        dve.wait_ge(gx_ready, min(w - 1, TILES))
                    nc.vector.tensor_scalar(xn[:, w % 2, :], summed[:, w % 2, :], mv[:, w % 2, 0:1],
                                            rstd[:, w % 2:w % 2 + 1], ALU.subtract, ALU.mult).then_inc(xn_ready, 1)

            def mix(t):
                u = t - 2
                if 0 <= u < UNITS:
                    dve.wait_ge(weighedT_ready, u + 1)
                    wt = dve_ps[:].rearrange("p (h x) -> p h x", x=SEQ)
                    nc.vector.reciprocal(rsum[:, u % 2, :].rearrange("p (h r) -> p h r", r=2),
                                         wt[:, :, 4 * HD:4 * HD + 2]).then_inc(rsum_ready, 1)
                    dve.wait_ge(rsum_ready, u + 1)
                    if u >= 2:
                        dve.wait_ge(mixedT_ready, u - 1)
                    for b in range(2):
                        q = slice(b * SEQ, (b + 1) * SEQ)
                        ins = nc.vector.tensor_tensor(
                            mixed[q, u % 2, :].rearrange("p (h r d) -> p h r d", h=HP, r=2),
                            wt[q, :, b * 2 * HD:(b + 1) * 2 * HD].rearrange("p h (r d) -> p h r d", r=2),
                            rsum[q, u % 2, :].rearrange("p (h r) -> p h r", r=2).unsqueeze(3).broadcast_to((SEQ, HP, 2, HD)),
                            ALU.mult)
                    ins.then_inc(mixed_ready, 1)

            for t in range(UNITS):
                maximum(t)
                residual(t)
                side_stage(t)
                shift(t)
                if t == 0:
                    spread_first(FIRST_SPREAD[2])
                    side_read(4)
                    side_read(5)
                mix(t)
                normalise(t)

            count = [0]

            def link(ins):
                count[0] += 1
                ins.then_inc(rchain, 1)
                dve.wait_ge(rchain, count[0])

            def over_experts(v):
                return v.unsqueeze(2).broadcast_to((P, TPC, E))

            def router_views(c):
                t = slice(c * TPC, (c + 1) * TPC)
                return [r_buf[:, i, t] for i in range(9)] + [r_one[:, i, t] for i in range(8)]

            ranks = rank[:].unsqueeze(1).broadcast_to((P, TPC, E))

            def router_logits(c):
                lg, sh, ex, pr, key, pick1, left, pick2, tmp, lmax, lsum, m1, dif, half_diff, den, gate1, gate2 = router_views(c)
                dve.wait_ge(logits_ready, c + 1)
                dve.wait_ge(small_in, 16 * 4)
                first = LOGITS + c * TPC * E
                nc.vector.tensor_tensor(lg, act_ps[:, first:first + TPC * E].rearrange("p (t e) -> p t e", e=E),
                                        rb_bc[:].unsqueeze(1).broadcast_to((P, TPC, E)), ALU.add).then_inc(logits_used, 1)
                dve.wait_ge(logits_used, c + 1)
                link(nc.vector.tensor_reduce(lmax, lg, AX.X, ALU.max))
                nc.vector.tensor_tensor(sh, lg, over_experts(lmax), ALU.subtract).then_inc(r_exp_in, 1)

            def router_picks(c):
                lg, sh, ex, pr, key, pick1, left, pick2, tmp, lmax, lsum, m1, dif, half_diff, den, gate1, gate2 = router_views(c)
                dve.wait_ge(r_exp, 2 * c + 1)
                link(nc.vector.tensor_reduce(lsum, ex, AX.X, ALU.add))
                link(nc.vector.reciprocal(den, lsum))
                link(nc.vector.tensor_tensor(pr, ex, over_experts(den), ALU.mult))
                link(nc.vector.tensor_reduce(m1, pr, AX.X, ALU.max))

                def pick(src, most, chosen):
                    link(nc.vector.tensor_tensor(key, src, over_experts(most), ALU.is_equal))
                    link(nc.vector.tensor_tensor(key, key, ranks, ALU.mult))
                    link(nc.vector.tensor_reduce(lmax, key, AX.X, ALU.max))
                    link(nc.vector.tensor_tensor(chosen, key, over_experts(lmax), ALU.is_equal))

                def flat(v):
                    return v.rearrange("p t e -> p (t e)")

                pick(pr, m1, pick1)
                link(nc.vector.scalar_tensor_tensor(flat(left), flat(pick1), -2.0, flat(pr), ALU.mult, ALU.add))
                link(nc.vector.tensor_reduce(lsum, left, AX.X, ALU.max))
                nc.vector.tensor_tensor(dif, lsum, m1, ALU.subtract).then_inc(r_exp_in, 1)
                pick(left, lsum, pick2)

            def router_gates(c):
                lg, sh, ex, pr, key, pick1, left, pick2, tmp, lmax, lsum, m1, dif, half_diff, den, gate1, gate2 = router_views(c)
                t = slice(c * TPC, (c + 1) * TPC)
                dve.wait_ge(r_exp, 2 * c + 2)
                nc.vector.tensor_scalar(gate1, half_diff, 0.5, 0.5, ALU.mult, ALU.add)
                link(nc.vector.tensor_scalar(gate2, half_diff, -0.5, 0.5, ALU.mult, ALU.add))
                link(nc.vector.tensor_tensor(pick1, pick1, over_experts(gate1), ALU.mult))
                link(nc.vector.tensor_tensor(tmp, pick2, over_experts(gate2), ALU.mult))
                link(nc.vector.tensor_tensor(gate[:, t], pick1, tmp, ALU.add))
                nc.vector.tensor_copy(gate_parts[:, t, 0, :], gate[:, t]).then_inc(gate_parts_ready, 1)
                dve.wait_ge(gate_parts_ready, 2 * c + 1)
                nc.vector.tensor_tensor(gate_parts[:, t, 1, :], gate[:, t], gate_parts[:, t, 0, :].bitcast(F32),
                                        ALU.subtract).then_inc(gate_parts_ready, 1)

            def remainder(n):
                dve.wait_ge(h_hi_ready, n + 1)
                slot = n % (2 * FC)
                nc.vector.tensor_tensor(h_lo[:, slot, :], h_raw[:, n % 4, :], h_hi[:, slot, :].bitcast(F32),
                                        ALU.subtract).then_inc(h_lo_ready, 1)

            def add_expert(g):
                c, e = g // E, g % E
                dve.wait_ge(gate_all_ready, g + 1)
                halves = 2 if g == STEPS - 1 else 1
                if e > 0:
                    dve.wait_ge(acc_ready, g)
                for half in range(halves):
                    w = CH // halves
                    t = slice(half * w, (half + 1) * w)
                    tok = slice(c * CH + half * w, c * CH + (half + 1) * w)
                    dve.wait_ge(down_ready, g + half + 1)
                    nc.vector.scalar_tensor_tensor(term[:, g % 2, t], probsT_ps[:, (g + half) % 2, t],
                                                   bias_cols[:, NB1 + e:NB1 + e + 1], gate_all[:, g % 2, t],
                                                   ALU.add, ALU.mult).then_inc(term_ready, 1)
                    dve.wait_ge(term_ready, g + half + 1)
                    nc.vector.tensor_tensor(acc[:, tok], term[:, g % 2, t], (yT[:, 1] if e == 0 else acc)[:, tok],
                                            ALU.add).then_inc(acc_ready, 1)

            l3 = [0]

            def link3(ins):
                l3[0] += 1
                ins.then_inc(l3chain, 1)

            def statistics(p):
                i0, n = PARTS[p]
                z = summed_bank(p).rearrange("p (t d) -> p t d", d=D)[:, 0:n, :]
                dve.wait_ge(accT_ready, p + 1)
                if p < LATE - 1:
                    nc.vector.tensor_copy(normed[:, i0:i0 + n, :], z).then_inc(accT_used, 1)
                    dve.wait_ge(accT_used, p + 1)
                    z = normed[:, i0:i0 + n, :]
                for j in range(n):
                    link3(nc.vector.bn_stats(st3[:, i0 + j, :], z[:, j, :]))
                dve.wait_ge(l3chain, l3[0])
                for i in range(i0, i0 + n):
                    link3(nc.vector.bn_aggr(mv3[:, i, :], st3[:, i, :]))
                dve.wait_ge(l3chain, l3[0])
                nc.vector.tensor_scalar(ve3[:, i0:i0 + n], mv3[:, i0:i0 + n, 1], EPS, None, ALU.add).then_inc(ve3_ready, 1)
                return z

            def center(p, z):
                i0, n = PARTS[p]
                for j in range(n):
                    link3(nc.vector.scalar_tensor_tensor(normed[:, i0 + j, :], z[:, j, :], mv3[:, i0 + j, 0:1], bc["g2"][:],
                                                         ALU.subtract, ALU.mult))
                return l3[0]

            def finish(p, centered):
                i0, n = PARTS[p]
                dve.wait_ge(rstd3_ready, p + 1)
                dve.wait_ge(l3chain, centered)
                for j in range(n):
                    ins = nc.vector.scalar_tensor_tensor(y3[:, i0 + j, :], normed[:, i0 + j, :], rstd3[:, i0 + j:i0 + j + 1],
                                                         bc["b2"][:], ALU.mult, ALU.add)
                ins.then_inc(y_ready[p], 1)

            router_logits(0)
            residual(UNITS)
            mix(UNITS)
            router_picks(0)
            normalise(UNITS)
            residual(UNITS + 1)
            mix(UNITS + 1)
            router_gates(0)
            normalise(UNITS + 1)
            residual(UNITS + 2)
            remainder(0)
            remainder(1)
            normalise(UNITS + 2)
            remainder(2)
            remainder(3)
            remainder(4)
            remainder(5)
            remainder(6)
            remainder(7)
            add_expert(0)
            router_logits(1)

            for g in range(2, STEPS):
                for n in range(g * FC, (g + 1) * FC):
                    remainder(n)
                add_expert(g - 1)
                if g == EXP1_STEP:
                    router_picks(1)
                if g == EXP2_STEP:
                    router_gates(1)
                if g == E + 1:
                    z0 = statistics(0)
                if g == E + 2:
                    finish(0, center(0, z0))
            add_expert(STEPS - 1)
            z1 = statistics(1)
            z2 = statistics(2)
            centered = [center(1, z1), center(2, z2)]
            finish(1, centered[0])
            finish(2, centered[1])

        @block.gpsimd
        def _(pool):
            gc = [0]

            def link(ins):
                gc[0] += 1
                ins.then_inc(chain_g, 1)
                pool.wait_ge(chain_g, gc[0])

            link(nc.gpsimd.memset(own_head[:], 1.0))
            link(nc.gpsimd.affine_select(out=own_head[:], in_=own_head[:], compare_op=ALU.is_ge, fill=0.0, base=0,
                                         pattern=[[-HD, HEADS]], channel_multiplier=1))
            nc.gpsimd.affine_select(out=own_head[:], in_=own_head[:], compare_op=ALU.is_ge, fill=0.0, base=HD - 1,
                                    pattern=[[HD, HEADS]], channel_multiplier=-1).then_inc(consts, 1)
            pool.wait_ge(consts, 1)
            link(nc.gpsimd.memset(ident[:], 0.0))
            nc.gpsimd.affine_select(out=ident[:], in_=ident[:], compare_op=ALU.not_equal, fill=1.0, base=0,
                                    pattern=[[-1, P]], channel_multiplier=1).then_inc(consts, 1)
            pool.wait_ge(consts, 2)
            nc.gpsimd.tensor_copy(ident_bf[:], ident[:]).then_inc(consts, 1)
            pool.wait_ge(consts, 3)
            link(nc.gpsimd.memset(mask_bf[:], 0.0))
            for b in range(2):
                m = mask_bf[b * SEQ:(b + 1) * SEQ, :].rearrange("p (h k) -> p h k", k=SEQ)
                ins = nc.gpsimd.affine_select(out=m, in_=m, compare_op=ALU.is_ge, fill=MASKED, base=0,
                                              pattern=[[0, HP], [-1, SEQ]], channel_multiplier=1)
                if b == 0:
                    link(ins)
            ins.then_inc(consts, 1)
            pool.wait_ge(consts, 4)
            nc.gpsimd.memset(spread[:, 1, :], 0.0).then_inc(zeroed, 1)
            pool.dma_start(bias_rows[0:NB1, :], b1.rearrange("e (k f) -> (e k) f", f=P)).then_inc(bias_in, 16)
            pool.dma_start(bias_rows[NB1:NB1 + E, :], b2).then_inc(bias_in, 16)
            pool.dma_start(bc["g2"][:], ln[2][0].partition_broadcast(P)).then_inc(small_in, 16)
            pool.dma_start(bc["b2"][:], ln[2][1].partition_broadcast(P)).then_inc(small_in, 16)
            pool.dma_start(rb_bc[:], router_b.partition_broadcast(P)).then_inc(small_in, 16)
            pool.dma_start(rw_sb[:], router_w).then_inc(small_in, 16)
            nc.gpsimd.memset(neg_half[:], -0.5).then_inc(consts, 1)
            pool.wait_ge(src_in[0][0], 16)
            pool.wait_ge(src_in[0][1], 16)
            pool.wait_ge(bo0_in, 16)
            nc.gpsimd.tensor_tensor(res[:, 0], x_sb[:], bc["bo0"][:].unsqueeze(1).broadcast_to((P, TILES, D)),
                                    ALU.add).then_inc(res0_ready, 1)
            for e in range(E):
                link(nc.gpsimd.memset(rank[:, e:e + 1], float(E - e)))
            blank = yT[0:2 * E, 1, :].rearrange("p (e m) -> p e m", m=P)
            link(nc.gpsimd.memset(blank, 0.0))
            link(nc.gpsimd.affine_select(out=blank, in_=blank, compare_op=ALU.not_equal, fill=1.0, base=0,
                                         pattern=[[-1, E], [0, P]], channel_multiplier=1))
            nc.gpsimd.affine_select(out=select[:], in_=blank, compare_op=ALU.not_equal, fill=1.0, base=-E,
                                    pattern=[[-1, E], [0, P]], channel_multiplier=1).then_inc(select_ready, 1)
            pool.wait_ge(lnp_in, 16 * 7)
            link(nc.gpsimd.tensor_tensor(bc["bo1"][:], bc["b0"][:], bc["bo1"][:], ALU.add))
            pool.wait_ge(consts, 5)

            def split_input(tile):
                pool.wait_ge(yT_ready, TILES + tile + 1)
                c = slice(tile * P, (tile + 1) * P)
                nc.gpsimd.tensor_copy(y2T_hi[:, c], yT[:, 1, c]).then_inc(y2T_hi_ready, 1)
                pool.wait_ge(y2T_hi_ready, tile + 1)
                nc.gpsimd.tensor_tensor(y2T_lo[:, c], yT[:, 1, c], y2T_hi[:, c].bitcast(F32),
                                        ALU.subtract).then_inc(y2T_lo_ready, 1)

            def w2_remainder(e):
                pool.wait_ge(w2_hi_ready, e + 1)
                nc.gpsimd.tensor_tensor(w2_lo[:, e].rearrange("p k d -> p (k d)"), raw(E + e),
                                        w2_hi[:, e].bitcast(F32).rearrange("p k d -> p (k d)"),
                                        ALU.subtract).then_inc(w2_lo_ready, 1)

            nc.gpsimd.memset(vals[:, 1].rearrange("p t h v -> p (t h v)"), 0.0).then_inc(vals_zeroed[1], 1)
            pool.wait_ge(vals_zeroed[1], 1)
            for par in range(2):
                nc.gpsimd.memset(vals[par * SEQ:(par + 1) * SEQ, 1, :, :, 4 * HD + par], 1.0).then_inc(vals_zeroed[1], 1)
                pool.wait_ge(vals_zeroed[1], par + 2)
            for u in range(UNITS):
                n, tile = u // TILES, u % TILES
                pool.wait_ge(veps_ready, u + 1)
                nc.gpsimd.tensor_tensor(rstd[:, u % 2:u % 2 + 1], veps[:, u % 2:u % 2 + 1], neg_half[:, 0:1],
                                        ALU.pow).then_inc(rstd_ready, 1)
                if n == 0:
                    pool.wait_ge(xn_ready, u + 1)
                    nc.gpsimd.tensor_tensor(gx[:], xn[:, u % 2, :], bc["g0"][:], ALU.mult).then_inc(gx_ready, 1)
                    pool.wait_ge(gx_ready, u + 1)
                    nc.gpsimd.tensor_tensor(res[:, 1, tile, :], gx[:], bc["bo1"][:], ALU.add).then_inc(res_ready, 1)
                    pool.wait_ge(w1_hi_ready, tile + 1)
                    nc.gpsimd.tensor_tensor(w1_lo[:, tile, :], raw(tile), w1_hi[:, tile, :].bitcast(F32),
                                            ALU.subtract).then_inc(w1_lo_ready, 1)
                if u > TILES:
                    split_input(tile - 1)
                    if tile < TPC:
                        w2_remainder(tile - 1)
            split_input(TILES - 1)
            for e in range(TPC - 1, E):
                w2_remainder(e)

            def deviation(p):
                i0, n = PARTS[p]
                pool.wait_ge(ve3_ready, p + 1)
                nc.gpsimd.tensor_tensor(rstd3[:, i0:i0 + n], ve3[:, i0:i0 + n], neg_half[:, 0:n],
                                        ALU.pow).then_inc(rstd3_ready, 1)

            for p in range(len(PARTS)):
                deviation(p)


_NAMES = ["x", "ctx_1024"] + [
    "L0_xattn_" + n for n in (
        "sa_wq sa_bq sa_wk sa_bk sa_wv sa_bv sa_wo sa_bo ca_wq ca_bq ca_wk ca_bk ca_wv ca_bv ca_wo ca_bo "
        "ln1_g ln1_b ln2_g ln2_b ln3_g ln3_b router_w router_b e_w1 e_b1 e_w2 e_b2").split()]


def kernel(**inputs):
    import numpy as np
    import concourse.bacc as bacc
    from concourse.bass_utils import run_bass_kernel_spmd

    nc = bacc.Bacc("TRN2", target_bir_lowering=False, num_devices=1)
    arrays, ap = {}, {}
    for name in _NAMES:
        a = np.ascontiguousarray(inputs[name])
        arrays[f"in_{name}"] = a
        ap[name.replace("L0_xattn_", "")] = nc.dram_tensor(
            f"in_{name}", a.shape, mybir.dt.from_np(a.dtype), kind="ExternalInput").ap()
    shape = inputs["x"].shape
    out = nc.dram_tensor("out_0", shape, F32, kind="ExternalOutput").ap()
    att = [{n: ap[f"{a}_{n}"] for n in ("wq", "bq", "wk", "bk", "wv", "bv", "wo", "bo")} for a in ("sa", "ca")]
    build_decoder_layer(nc, ap["x"], ap["ctx_1024"], att[0], att[1],
                        [(ap[f"ln{i}_g"], ap[f"ln{i}_b"]) for i in (1, 2, 3)],
                        ap["router_w"], ap["router_b"], ap["e_w1"], ap["e_b1"], ap["e_w2"], ap["e_b2"], out)
    r = run_bass_kernel_spmd(nc, [arrays], core_ids=[0])
    return r.results[0]["out_0"]
```
